# Optimizing a Trainium2 kernel written in Bass

```python
import numpy as np
import jax
import jax.numpy as jnp

def _softmax(x, axis=-1):
    return jax.nn.softmax(x, axis=axis)

def _gelu(x):
    return jax.nn.gelu(x, approximate=True)

def _silu(x):
    return jax.nn.silu(x)

def _sigmoid(x):
    return jax.nn.sigmoid(x)

def _layernorm(x, axis=-1, eps=1e-05):
    m = jnp.mean(x, axis=axis, keepdims=True)
    v = jnp.var(x, axis=axis, keepdims=True)
    return (x - m) / jnp.sqrt(v + eps)

def _scatter_add(tgt, idx, src, axis=0):
    return tgt.at[idx].add(src)

def _segment_sum(src, seg, n):
    return jax.ops.segment_sum(src, seg, n)
kernel_name = 'mk_sandwich_d2_jaxref_r4_773f9b'

def setup_inputs(seed: int=0):
    np.random.seed(seed)
    _w = jnp.asarray

    def _L0_attn_setup():
        import jax, jax.numpy as jnp
        import numpy as np
        D_MODEL = 512
        EXPAND = 2
        INNER = EXPAND * D_MODEL
        HEADDIM = 64
        NHEADS = INNER // HEADDIM
        D_CONV = 4
        BATCH, SEQLEN = (2, 1024)

        def _dw_causal_conv_silu(x, w, b):
            K = w.shape[1]
            L = x.shape[1]
            xp = jnp.pad(x, ((0, 0), (K - 1, 0), (0, 0)))
            y = b
            for k in range(K):
                y = y + w[:, k] * xp[:, k:k + L, :]
            return jax.nn.silu(y)

        def _diag_ssm_scan(a, u):

            def comb(c1, c2):
                a1, b1 = c1
                a2, b2 = c2
                return (a1 * a2, a2 * b1 + b2)
            _, s = jax.lax.associative_scan(comb, (a, u), axis=1)
            return s
        key = jax.random.key(seed)
        ks = jax.random.split(key, 12)
        f32 = jnp.float32
        return {'hidden_states': jax.random.normal(ks[0], (BATCH, SEQLEN, D_MODEL), f32), 'in_proj_w': jax.random.normal(ks[1], (INNER, D_MODEL), f32) * 0.02, 'gate_proj_w': jax.random.normal(ks[2], (INNER, D_MODEL), f32) * 0.02, 'out_proj_w': jax.random.normal(ks[3], (D_MODEL, INNER), f32) * 0.02, 'conv_weight': jax.random.normal(ks[4], (INNER, D_CONV), f32) * 0.02, 'conv_bias': jnp.zeros((INNER,), f32), 'dt_w': jax.random.normal(ks[5], (NHEADS, HEADDIM), f32) * 0.02, 'dt_b': jnp.zeros((NHEADS,), f32), 'A_log': jax.random.normal(ks[6], (NHEADS, HEADDIM), f32) * 0.1, 'B': jax.random.normal(ks[7], (NHEADS, HEADDIM), f32) * 0.02, 'C': jax.random.normal(ks[8], (NHEADS, HEADDIM), f32) * 0.02, 'D': jnp.ones((NHEADS, HEADDIM), f32)}
    _L0_attn_in = _L0_attn_setup()

    def _L0_ffn_setup():
        import jax, jax.numpy as jnp
        import numpy as np
        TOP_K = 2
        key = jax.random.key(seed)
        ks = jax.random.split(key, 6)
        B, S, H, F, E = (1, 512, 512, 352, 8)
        Fs = 2 * F
        std = jnp.float32(0.02)
        return {'hidden_states': jax.random.normal(ks[0], (B, S, H), jnp.float32), 'gate_weight': jax.random.normal(ks[1], (E, H), jnp.float32) * std, 'gate_up_weights': jax.random.normal(ks[2], (E, 2 * F, H), jnp.float32) * std, 'down_weights': jax.random.normal(ks[3], (E, H, F), jnp.float32) * std, 'shared_gate_up': jax.random.normal(ks[4], (2 * Fs, H), jnp.float32) * std, 'shared_down': jax.random.normal(ks[5], (H, Fs), jnp.float32) * std}
    _L0_ffn_in = _L0_ffn_setup()

    def _L1_attn_setup():
        import jax, jax.numpy as jnp
        import numpy as np
        H = 512
        NH = 16
        D = 128
        K = 4

        def _causal_depthwise_conv(x, w, b):
            S = x.shape[1]
            xp = jnp.pad(x, ((0, 0), (K - 1, 0), (0, 0)))
            y = b
            for j in range(K):
                y = y + xp[:, j:j + S, :] * w[:, j]
            return y

        def _forward(x, Wq, Wk, Wv, Wa, ba, Wb, bb, Wg, Wo, qcw, qcb, kcw, kcb, vcw, vcb, ln_w, ln_b):
            B, S, _ = x.shape
            q = _causal_depthwise_conv(x @ Wq, qcw, qcb)
            k = _causal_depthwise_conv(x @ Wk, kcw, kcb)
            v = _causal_depthwise_conv(x @ Wv, vcw, vcb)
            q = jax.nn.silu(q).reshape(B, S, NH, D)
            k = jax.nn.silu(k).reshape(B, S, NH, D) * D ** (-0.5)
            v = jax.nn.silu(v).reshape(B, S, NH, D)
            alpha = jax.nn.sigmoid(x @ Wa + ba)
            beta = jax.nn.sigmoid(x @ Wb + bb)
            qt = jnp.moveaxis(q, 1, 0)
            kt = jnp.moveaxis(k, 1, 0)
            vt = jnp.moveaxis(v, 1, 0)
            at = jnp.moveaxis(alpha, 1, 0)
            bt = jnp.moveaxis(beta, 1, 0)

            def step(St, inp):
                q_, k_, v_, a_, b_ = inp
                sk = jnp.einsum('bhij,bhj->bhi', St, k_)
                err = sk - v_
                Sn = a_[..., None, None] * St - b_[..., None, None] * err[..., None] * k_[..., None, :]
                o_ = jnp.einsum('bhij,bhj->bhi', Sn, q_)
                return (Sn, o_)
            S0 = jnp.zeros((B, NH, D, D), dtype=x.dtype)
            _, o = jax.lax.scan(step, S0, (qt, kt, vt, at, bt))
            o = jnp.moveaxis(o, 0, 1)
            mu = jnp.mean(o, axis=-1, keepdims=True)
            var = jnp.mean(jnp.square(o - mu), axis=-1, keepdims=True)
            o = (o - mu) * jax.lax.rsqrt(var + 1e-05) * ln_w + ln_b
            g = jax.nn.sigmoid(x @ Wg).reshape(B, S, NH, D)
            o = (o * g).reshape(B, S, NH * D)
            return o @ Wo
        key = jax.random.key(seed)
        ks = jax.random.split(key, 18)
        s = 0.02
        B, S = (2, 512)
        return {'x': jax.random.normal(ks[0], (B, S, H), dtype=jnp.float32), 'Wq': jax.random.normal(ks[1], (H, NH * D), dtype=jnp.float32) * s, 'Wk': jax.random.normal(ks[2], (H, NH * D), dtype=jnp.float32) * s, 'Wv': jax.random.normal(ks[3], (H, NH * D), dtype=jnp.float32) * s, 'Wa': jax.random.normal(ks[4], (H, NH), dtype=jnp.float32) * s, 'ba': jax.random.normal(ks[5], (NH,), dtype=jnp.float32) * s, 'Wb': jax.random.normal(ks[6], (H, NH), dtype=jnp.float32) * s, 'bb': jax.random.normal(ks[7], (NH,), dtype=jnp.float32) * s, 'Wg': jax.random.normal(ks[8], (H, NH * D), dtype=jnp.float32) * s, 'Wo': jax.random.normal(ks[9], (NH * D, H), dtype=jnp.float32) * s, 'qcw': jax.random.normal(ks[10], (NH * D, K), dtype=jnp.float32) * s, 'qcb': jax.random.normal(ks[11], (NH * D,), dtype=jnp.float32) * s, 'kcw': jax.random.normal(ks[12], (NH * D, K), dtype=jnp.float32) * s, 'kcb': jax.random.normal(ks[13], (NH * D,), dtype=jnp.float32) * s, 'vcw': jax.random.normal(ks[14], (NH * D, K), dtype=jnp.float32) * s, 'vcb': jax.random.normal(ks[15], (NH * D,), dtype=jnp.float32) * s, 'ln_w': jnp.ones((D,), dtype=jnp.float32), 'ln_b': jnp.zeros((D,), dtype=jnp.float32)}
    _L1_attn_in = _L1_attn_setup()

    def _L1_ffn_setup():
        import jax, jax.numpy as jnp
        import numpy as np
        B, S, D, E, TOPK, H = (8, 512, 512, 8, 2, 16)
        DH = D // H
        FH = D // H
        ROUTE_LEN = 512
        key = jax.random.key(seed)
        ks = jax.random.split(key, 8)
        s = 0.02
        return {'x': jax.random.normal(ks[0], (B, S, D), jnp.float32), 'switch_w': jax.random.normal(ks[1], (E, D * ROUTE_LEN), jnp.float32) * s, 'switch_b': jnp.zeros((E,), jnp.float32), 'w1': jax.random.normal(ks[2], (E, FH, DH), jnp.float32) * s, 'b1': jnp.zeros((E, FH), jnp.float32), 'w2': jax.random.normal(ks[3], (E, DH, FH), jnp.float32) * s, 'b2': jnp.zeros((E, DH), jnp.float32), 'w3': jax.random.normal(ks[4], (D, D), jnp.float32) * s, 'b3': jnp.zeros((D,), jnp.float32)}
    _L1_ffn_in = _L1_ffn_setup()
    _d = {'L0_attn_hidden_states': _L0_attn_in['hidden_states'], 'L0_attn_in_proj_w': _L0_attn_in['in_proj_w'], 'L0_attn_gate_proj_w': _L0_attn_in['gate_proj_w'], 'L0_attn_out_proj_w': _L0_attn_in['out_proj_w'], 'L0_attn_conv_weight': _L0_attn_in['conv_weight'], 'L0_attn_conv_bias': _L0_attn_in['conv_bias'], 'L0_attn_dt_w': _L0_attn_in['dt_w'], 'L0_attn_dt_b': _L0_attn_in['dt_b'], 'L0_attn_A_log': _L0_attn_in['A_log'], 'L0_attn_B': _L0_attn_in['B'], 'L0_attn_C': _L0_attn_in['C'], 'L0_attn_D': _L0_attn_in['D'], 'L0_ffn_gate_weight': _L0_ffn_in['gate_weight'], 'L0_ffn_gate_up_weights': _L0_ffn_in['gate_up_weights'], 'L0_ffn_down_weights': _L0_ffn_in['down_weights'], 'L0_ffn_shared_gate_up': _L0_ffn_in['shared_gate_up'], 'L0_ffn_shared_down': _L0_ffn_in['shared_down'], 'L1_attn_Wq': _L1_attn_in['Wq'], 'L1_attn_Wk': _L1_attn_in['Wk'], 'L1_attn_Wv': _L1_attn_in['Wv'], 'L1_attn_Wa': _L1_attn_in['Wa'], 'L1_attn_ba': _L1_attn_in['ba'], 'L1_attn_Wb': _L1_attn_in['Wb'], 'L1_attn_bb': _L1_attn_in['bb'], 'L1_attn_Wg': _L1_attn_in['Wg'], 'L1_attn_Wo': _L1_attn_in['Wo'], 'L1_attn_qcw': _L1_attn_in['qcw'], 'L1_attn_qcb': _L1_attn_in['qcb'], 'L1_attn_kcw': _L1_attn_in['kcw'], 'L1_attn_kcb': _L1_attn_in['kcb'], 'L1_attn_vcw': _L1_attn_in['vcw'], 'L1_attn_vcb': _L1_attn_in['vcb'], 'L1_attn_ln_w': _L1_attn_in['ln_w'], 'L1_attn_ln_b': _L1_attn_in['ln_b'], 'L1_ffn_switch_w': _L1_ffn_in['switch_w'], 'L1_ffn_switch_b': _L1_ffn_in['switch_b'], 'L1_ffn_w1': _L1_ffn_in['w1'], 'L1_ffn_b1': _L1_ffn_in['b1'], 'L1_ffn_w2': _L1_ffn_in['w2'], 'L1_ffn_b2': _L1_ffn_in['b2'], 'L1_ffn_w3': _L1_ffn_in['w3'], 'L1_ffn_b3': _L1_ffn_in['b3']}
    _x0 = _d['L0_attn_hidden_states']
    _d['L0_attn_hidden_states'] = jax.random.normal(jax.random.fold_in(jax.random.key(seed), 1), (4, 512, 512), dtype=_x0.dtype)
    del _x0
    return _d

def reference(L0_attn_hidden_states, L0_attn_in_proj_w, L0_attn_gate_proj_w, L0_attn_out_proj_w, L0_attn_conv_weight, L0_attn_conv_bias, L0_attn_dt_w, L0_attn_dt_b, L0_attn_A_log, L0_attn_B, L0_attn_C, L0_attn_D, L0_ffn_gate_weight, L0_ffn_gate_up_weights, L0_ffn_down_weights, L0_ffn_shared_gate_up, L0_ffn_shared_down, L1_attn_Wq, L1_attn_Wk, L1_attn_Wv, L1_attn_Wa, L1_attn_ba, L1_attn_Wb, L1_attn_bb, L1_attn_Wg, L1_attn_Wo, L1_attn_qcw, L1_attn_qcb, L1_attn_kcw, L1_attn_kcb, L1_attn_vcw, L1_attn_vcb, L1_attn_ln_w, L1_attn_ln_b, L1_ffn_switch_w, L1_ffn_switch_b, L1_ffn_w1, L1_ffn_b1, L1_ffn_w2, L1_ffn_b2, L1_ffn_w3, L1_ffn_b3):

    def _L0_attn_ref(hidden_states, in_proj_w, gate_proj_w, out_proj_w, conv_weight, conv_bias, dt_w, dt_b, A_log, B, C, D):
        import jax, jax.numpy as jnp
        import numpy as np
        D_MODEL = 512
        EXPAND = 2
        INNER = EXPAND * D_MODEL
        HEADDIM = 64
        NHEADS = INNER // HEADDIM
        D_CONV = 4
        BATCH, SEQLEN = (2, 1024)

        def _dw_causal_conv_silu(x, w, b):
            K = w.shape[1]
            L = x.shape[1]
            xp = jnp.pad(x, ((0, 0), (K - 1, 0), (0, 0)))
            y = b
            for k in range(K):
                y = y + w[:, k] * xp[:, k:k + L, :]
            return jax.nn.silu(y)

        def _diag_ssm_scan(a, u):

            def comb(c1, c2):
                a1, b1 = c1
                a2, b2 = c2
                return (a1 * a2, a2 * b1 + b2)
            _, s = jax.lax.associative_scan(comb, (a, u), axis=1)
            return s
        batch, seqlen, _ = hidden_states.shape
        projected = jnp.einsum('bld,cd->blc', hidden_states, in_proj_w)
        conv_out = _dw_causal_conv_silu(projected, conv_weight, conv_bias)
        gate = jax.nn.sigmoid(jnp.einsum('bld,cd->blc', hidden_states, gate_proj_w))
        X = conv_out.reshape(batch, seqlen, NHEADS, HEADDIM)
        dt = jax.nn.softplus(jnp.einsum('blhp,hp->blh', X, dt_w) + dt_b)
        A = -jnp.exp(A_log)
        a = jnp.exp(dt[..., None] * A)
        u = dt[..., None] * B * X
        s = _diag_ssm_scan(a, u)
        y = C * s + D * X
        combined = y.reshape(batch, seqlen, INNER) * gate
        return jnp.einsum('blc,dc->bld', combined, out_proj_w)

    def _L0_ffn_ref(hidden_states, gate_weight, gate_up_weights, down_weights, shared_gate_up, shared_down):
        import jax, jax.numpy as jnp
        import numpy as np
        TOP_K = 2
        B, S, H = hidden_states.shape
        E, twoF, _ = gate_up_weights.shape
        F = twoF // 2
        T = B * S
        x = hidden_states.reshape(T, H)
        logits = x @ gate_weight.T
        scores = jax.nn.softmax(logits, axis=-1)
        topk_w, topk_idx = jax.lax.top_k(scores, TOP_K)
        combine = jnp.zeros((T, E), x.dtype).at[jnp.arange(T)[:, None], topk_idx].add(topk_w)
        gu = jnp.einsum('th,efh->tef', x, gate_up_weights)
        act = jax.nn.silu(gu[..., :F]) * gu[..., F:]
        y = jnp.einsum('tef,te,ehf->th', act, combine, down_weights)
        Fs = shared_gate_up.shape[0] // 2
        sgu = x @ shared_gate_up.T
        sact = jax.nn.silu(sgu[:, :Fs]) * sgu[:, Fs:]
        y = y + sact @ shared_down.T
        return y.reshape(B, S, H)

    def _L1_attn_ref(x, Wq, Wk, Wv, Wa, ba, Wb, bb, Wg, Wo, qcw, qcb, kcw, kcb, vcw, vcb, ln_w, ln_b):
        import jax, jax.numpy as jnp
        import numpy as np
        H = 512
        NH = 16
        D = 128
        K = 4

        def _causal_depthwise_conv(x, w, b):
            S = x.shape[1]
            xp = jnp.pad(x, ((0, 0), (K - 1, 0), (0, 0)))
            y = b
            for j in range(K):
                y = y + xp[:, j:j + S, :] * w[:, j]
            return y

        def _forward(x, Wq, Wk, Wv, Wa, ba, Wb, bb, Wg, Wo, qcw, qcb, kcw, kcb, vcw, vcb, ln_w, ln_b):
            B, S, _ = x.shape
            q = _causal_depthwise_conv(x @ Wq, qcw, qcb)
            k = _causal_depthwise_conv(x @ Wk, kcw, kcb)
            v = _causal_depthwise_conv(x @ Wv, vcw, vcb)
            q = jax.nn.silu(q).reshape(B, S, NH, D)
            k = jax.nn.silu(k).reshape(B, S, NH, D) * D ** (-0.5)
            v = jax.nn.silu(v).reshape(B, S, NH, D)
            alpha = jax.nn.sigmoid(x @ Wa + ba)
            beta = jax.nn.sigmoid(x @ Wb + bb)
            qt = jnp.moveaxis(q, 1, 0)
            kt = jnp.moveaxis(k, 1, 0)
            vt = jnp.moveaxis(v, 1, 0)
            at = jnp.moveaxis(alpha, 1, 0)
            bt = jnp.moveaxis(beta, 1, 0)

            def step(St, inp):
                q_, k_, v_, a_, b_ = inp
                sk = jnp.einsum('bhij,bhj->bhi', St, k_)
                err = sk - v_
                Sn = a_[..., None, None] * St - b_[..., None, None] * err[..., None] * k_[..., None, :]
                o_ = jnp.einsum('bhij,bhj->bhi', Sn, q_)
                return (Sn, o_)
            S0 = jnp.zeros((B, NH, D, D), dtype=x.dtype)
            _, o = jax.lax.scan(step, S0, (qt, kt, vt, at, bt))
            o = jnp.moveaxis(o, 0, 1)
            mu = jnp.mean(o, axis=-1, keepdims=True)
            var = jnp.mean(jnp.square(o - mu), axis=-1, keepdims=True)
            o = (o - mu) * jax.lax.rsqrt(var + 1e-05) * ln_w + ln_b
            g = jax.nn.sigmoid(x @ Wg).reshape(B, S, NH, D)
            o = (o * g).reshape(B, S, NH * D)
            return o @ Wo
        return _forward(x, Wq, Wk, Wv, Wa, ba, Wb, bb, Wg, Wo, qcw, qcb, kcw, kcb, vcw, vcb, ln_w, ln_b)

    def _L1_ffn_ref(x, switch_w, switch_b, w1, b1, w2, b2, w3, b3):
        import jax, jax.numpy as jnp
        import numpy as np
        B, S, D, E, TOPK, H = (8, 512, 512, 8, 2, 16)
        DH = D // H
        FH = D // H
        ROUTE_LEN = 512
        b, s, d = x.shape
        x0 = x[:, :ROUTE_LEN].reshape(b, -1)
        logits = x0 @ switch_w.T + switch_b
        probs = jax.nn.softmax(logits, axis=-1)
        gate, top_idx = jax.lax.top_k(probs, TOPK)
        xh = x.reshape(b, s, H, DH).transpose(0, 2, 1, 3)
        w1s, b1s = (w1[top_idx], b1[top_idx])
        w2s, b2s = (w2[top_idx], b2[top_idx])
        h = jnp.einsum('bhsd,bkfd->bkhsf', xh, w1s) + b1s[:, :, None, None, :]
        h = jax.nn.gelu(h, approximate=False)
        o = jnp.einsum('bkhsf,bkdf->bkhsd', h, w2s) + b2s[:, :, None, None, :]
        o = (o * gate[:, :, None, None, None]).sum(axis=1)
        o = o.transpose(0, 2, 1, 3).reshape(b, s, d)
        out = x + o
        return out @ w3.T + b3
    x = L0_attn_hidden_states
    x = x + _layernorm(_L0_attn_ref(_layernorm(x, axis=-1), L0_attn_in_proj_w, L0_attn_gate_proj_w, L0_attn_out_proj_w, L0_attn_conv_weight, L0_attn_conv_bias, L0_attn_dt_w, L0_attn_dt_b, L0_attn_A_log, L0_attn_B, L0_attn_C, L0_attn_D), axis=-1)
    x = x + _layernorm(_L0_ffn_ref(_layernorm(x, axis=-1), L0_ffn_gate_weight, L0_ffn_gate_up_weights, L0_ffn_down_weights, L0_ffn_shared_gate_up, L0_ffn_shared_down), axis=-1)
    x = x + _layernorm(_L1_attn_ref(_layernorm(x, axis=-1), L1_attn_Wq, L1_attn_Wk, L1_attn_Wv, L1_attn_Wa, L1_attn_ba, L1_attn_Wb, L1_attn_bb, L1_attn_Wg, L1_attn_Wo, L1_attn_qcw, L1_attn_qcb, L1_attn_kcw, L1_attn_kcb, L1_attn_vcw, L1_attn_vcb, L1_attn_ln_w, L1_attn_ln_b), axis=-1)
    x = x + _layernorm(_L1_ffn_ref(_layernorm(x, axis=-1), L1_ffn_switch_w, L1_ffn_switch_b, L1_ffn_w1, L1_ffn_b1, L1_ffn_w2, L1_ffn_b2, L1_ffn_w3, L1_ffn_b3), axis=-1)
    return x

_drawn_inputs = setup_inputs


def setup_inputs(seed=0):
    import zlib

    import numpy as np

    out = dict(_drawn_inputs(seed))
    spreads = {'L0_attn_conv_bias': (0.0, 0.1),
     'L0_attn_dt_b': (0.0, 2.0),
     'L0_attn_D': (1.0, 0.2),
     'L1_attn_ln_w': (1.0, 0.6),
     'L1_attn_ln_b': (0.0, 0.1),
     'L1_ffn_switch_b': (0.0, 0.1),
     'L1_ffn_b1': (0.0, 0.8),
     'L1_ffn_b2': (0.0, 0.1),
     'L1_ffn_b3': (0.0, 0.1)}
    factors = {'L0_attn_dt_w': 200.0,
     'L0_attn_A_log': 8.0,
     'L0_attn_B': 8.0,
     'L0_attn_C': 8.0,
     'L1_attn_Wq': 8.0,
     'L1_attn_Wk': 8.0,
     'L1_attn_Wv': 8.0,
     'L1_attn_Wa': 8.0,
     'L1_attn_ba': 31.732,
     'L1_attn_Wb': 8.0,
     'L1_attn_bb': 49.245,
     'L1_attn_qcw': 8.0,
     'L1_attn_qcb': 8.0,
     'L1_attn_kcw': 8.0,
     'L1_attn_kcb': 8.0,
     'L1_attn_vcw': 8.0,
     'L1_attn_vcb': 8.0,
     'L1_ffn_w1': 8.0,
     'L1_ffn_w2': 8.0}
    for name, (base, spread) in spreads.items():
        noise = np.random.default_rng([zlib.crc32(name.encode()), seed]).standard_normal(out[name].shape)
        drawn = base * np.exp(spread * noise) if base else spread * noise
        out[name] = jnp.asarray(drawn.astype(out[name].dtype))
    for name, factor in factors.items():
        out[name] = (out[name] * factor).astype(out[name].dtype)
    return out
```

```python
from contextlib import ExitStack

import concourse.bass as bass
from concourse import mybir
from concourse.alu_op_type import AluOpType as ALU

ACT = mybir.ActivationFunctionType
AX = mybir.AxisListType
F32 = mybir.dt.float32
U32 = mybir.dt.uint32

P = 128
DM = 512
KD = DM // P
NB = 4
SEQ = 512
TPB = SEQ // P
NT = NB * TPB
EPS = 1e-5

INNER = 1024
CT = INNER // P
TAPS = 4

NE = 8
FE = 352
FT = [(0, 128), (128, 128), (256, 96)]
NSH = 2
NX = NE + NSH

NH = 16
DH = 128
HG = 4
NG = NH // HG
LEVELS = [2, 4, 8, 16, 32, 64]

FH = 32
NHF = 16


class Program:

    def __init__(self, nc, io):
        self.nc, self.io = nc, io
        self.lasting = ExitStack()
        self.waits_passed = self.lasting.enter_context(nc.semaphore("waits_passed"))
        self.phase_sems = []

    def sem(self, name):
        self.phase_sems.append(self.nc.alloc_semaphore(name=name))
        return self.phase_sems[-1]

    def retire_sems(self):
        with self.nc.Block() as block:
            @block.gpsimd
            def _(e):
                for s in self.phase_sems:
                    e.sem_clear(s)
        for s in self.phase_sems:
            self.nc.release_semaphore(s)
        self.phase_sems = []

    def sb(self, stack, name, shape, dt=F32):
        return stack.enter_context(self.nc.sbuf_tensor(name, shape, dt))

    def ps(self, stack, name, shape, dt=F32):
        return stack.enter_context(self.nc.psum_tensor(name, shape, dt))


class Norm:

    def __init__(self, pr, stack, tag):
        sb = lambda n, s: pr.sb(stack, f"{tag}_{n}", s)
        sem = lambda n: pr.sem(f"{tag}_{n}")
        self.x = sb("x", [P, TPB, DM])
        self.yn = sb("yn", [P, TPB, DM])
        self.st1, self.st2 = sb("st1", [P, TPB, 6]), sb("st2", [P, TPB, 6])
        self.mv1, self.mv2 = sb("mv1", [P, TPB, 2]), sb("mv2", [P, TPB, 2])
        self.ln1, self.ln2 = sb("ln1", [P, TPB]), sb("ln2", [P, TPB])
        self.rs1, self.rs2 = sb("rs1", [P, TPB]), sb("rs2", [P, TPB])
        self.waits_passed = pr.waits_passed
        self.x_loaded = sem("x_loaded")
        self.y_stats = sem("y_stats")
        self.y_mv = sem("y_mv")
        self.y_ln = sem("y_ln")
        self.y_rstd = sem("y_rstd")
        self.y_normed = sem("y_normed")
        self.x_new = sem("x_new")
        self.x_stored = sem("x_stored")
        self.x_stats = sem("x_stats")
        self.x_mv = sem("x_mv")
        self.x_ln = sem("x_ln")
        self.x_rstd = sem("x_rstd")
        self.x_normed = sem("x_normed")
        self.turned = sem("turned")
        self.xt_done = sem("xt_done")


def stand(e, passed):
    e.sem_inc(passed, 1)


def norm_sync(e, n, r, x_old, x_out):
    e.wait_ge(n.x_stored, 16 * r + 1)
    stand(e, n.waits_passed)
    e.wait_ge(n.x_normed, TPB * r + 1)
    stand(e, n.waits_passed)
    e.dma_start(n.x[:, :, :], x_old).then_inc(n.x_loaded, 16)
    e.wait_ge(n.x_new, TPB * r + TPB)
    stand(e, n.waits_passed)
    e.dma_start(x_out, n.x[:, :, :]).then_inc(n.x_stored, 16)


def norm_y_vector(e, n, r, y, wait_y):
    for c in range(TPB):
        wait_y(c)
        e.bn_stats(n.st1[:, c, :], y(c)).then_inc(n.y_stats, 1)
    for c in range(TPB):
        e.wait_ge(n.y_stats, TPB * r + c + 1)
        stand(e, n.waits_passed)
        e.bn_aggr(n.mv1[:, c, :], n.st1[:, c, :]).then_inc(n.y_mv, 1)
    e.wait_ge(n.turned, TPB * r + 1)
    e.wait_ge(n.y_rstd, r + 1)
    for c in range(TPB):
        e.tensor_scalar(n.yn[:, c, :], y(c), n.mv1[:, c, 0:1], n.rs1[:, c:c + 1],
                        ALU.subtract, ALU.mult).then_inc(n.y_normed, 1)
    e.wait_ge(n.x_loaded, 16 * r + 16)
    for c in range(TPB):
        e.wait_ge(n.y_normed, TPB * r + c + 1)
        e.tensor_tensor(n.x[:, c, :], n.x[:, c, :], n.yn[:, c, :], ALU.add).then_inc(n.x_new, 1)


def norm_x_vector(e, n, r, wait_x):
    for c in range(TPB):
        wait_x(c)
        e.bn_stats(n.st2[:, c, :], n.x[:, c, :]).then_inc(n.x_stats, 1)
    for c in range(TPB):
        e.wait_ge(n.x_stats, TPB * r + c + 1)
        stand(e, n.waits_passed)
        e.bn_aggr(n.mv2[:, c, :], n.st2[:, c, :]).then_inc(n.x_mv, 1)
    e.wait_ge(n.turned, TPB * r + 1)
    e.wait_ge(n.x_rstd, r + 1)
    for c in range(TPB):
        e.tensor_scalar(n.yn[:, c, :], n.x[:, c, :], n.mv2[:, c, 0:1], n.rs2[:, c:c + 1],
                        ALU.subtract, ALU.mult).then_inc(n.x_normed, 1)


def norm_y_scalar(e, n, r, eps):
    e.wait_ge(n.y_mv, TPB * r + TPB)
    e.activation(n.ln1[:, :], n.mv1[:, :, 1], ACT.Ln, bias=eps).then_inc(n.y_ln, 1)
    e.wait_ge(n.y_ln, r + 1)
    e.activation(n.rs1[:, :], n.ln1[:, :], ACT.Exp, scale=-0.5).then_inc(n.y_rstd, 1)


def norm_x_scalar(e, n, r, eps, turned, xt):
    e.wait_ge(n.x_mv, TPB * r + TPB)
    e.activation(n.ln2[:, :], n.mv2[:, :, 1], ACT.Ln, bias=eps).then_inc(n.x_ln, 1)
    e.wait_ge(n.x_ln, r + 1)
    e.activation(n.rs2[:, :], n.ln2[:, :], ACT.Exp, scale=-0.5).then_inc(n.x_rstd, 1)
    for c in range(TPB):
        e.wait_ge(n.turned, TPB * r + c + 2)
        e.activation(xt(c), turned[:, :, :], ACT.Copy).then_inc(n.xt_done, 1)


def norm_x_tensor(e, n, r, turned, ident):
    for c in range(TPB):
        e.wait_ge(n.x_normed, TPB * r + c + 2)
        e.wait_ge(n.xt_done, TPB * r + c + 1)
        for k in range(KD):
            mm = e.transpose(turned[:, k, :], n.yn[:, c, k * P:(k + 1) * P], ident)
        mm.then_inc(n.turned, 1)


def norm_start(e, n):
    for s in (n.x_stored, n.x_normed, n.turned, n.xt_done):
        e.sem_inc(s, 1)


def rows(dram, b):
    return dram[b].rearrange("(c p) d -> p c d", p=P)


def constants(pr, stack):
    c = {}
    c["ident"] = pr.sb(stack, "ident", [P, P])
    c["eps"] = pr.sb(stack, "eps", [P, 1])
    for name in ("ones", "before", "upto", "after"):
        c[name] = pr.sb(stack, name, [P, P])
    return c


def phase_first_norm(pr, con, XT):
    nc, io = pr.nc, pr.io
    with ExitStack() as st:
        n = Norm(pr, st, "n0")
        turned = pr.ps(st, "n0_tp", [P, KD, P])
        made = pr.sem("constants_made")
        block = st.enter_context(nc.Block())

        @block.sync
        def _(e):
            with e.Fori(0, NB) as b:
                e.wait_ge(n.x_normed, TPB * b + 1)
                stand(e, pr.waits_passed)
                e.dma_start(n.x[:, :, :], rows(io["x"], b)).then_inc(n.x_loaded, 16)

        @block.gpsimd
        def _(e):
            norm_start(e, n)
            e.memset(con["eps"][:, :], EPS).then_inc(made, 1)
            e.memset(con["ones"][:, :], 1.0).then_inc(made, 1)
            e.memset(con["ident"][:, :], 0.0).then_inc(made, 1)
            e.wait_ge(made, 3)
            e.affine_select(out=con["ident"][:, :], in_=con["ident"][:, :], compare_op=ALU.not_equal,
                            fill=1.0, base=0, pattern=[[-1, P]], channel_multiplier=1).then_inc(made, 1)

        @block.vector
        def _(e):
            with e.Fori(0, NB) as b:
                norm_x_vector(e, n, b, lambda c: e.wait_ge(n.x_loaded, 16 * b + 16))

        @block.scalar
        def _(e):
            e.wait_ge(made, 4)
            with e.Fori(0, NB) as b:
                norm_x_scalar(e, n, b, con["eps"][:, :], turned,
                              lambda c: XT[:, b, :, c * P:(c + 1) * P])

        @block.tensor
        def _(e):
            e.wait_ge(made, 4)
            with e.Fori(0, NB) as b:
                norm_x_tensor(e, n, b, turned, con["ident"][:, :])


def phase_ssm(pr, con, XT):
    nc, io = pr.nc, pr.io
    with ExitStack() as st:
        sb = lambda n, s: pr.sb(st, "a_" + n, s)
        ps = lambda n, s: pr.ps(st, "a_ps_" + n, s)
        sem = lambda n: pr.sem("a_" + n)
        n = Norm(pr, st, "a")
        w_in, w_gate = sb("w_in", [P, KD, INNER]), sb("w_gate", [P, KD, INNER])
        w_out = sb("w_out", [P, CT, DM])
        conv_w, conv_b = sb("conv_w", [P, CT, TAPS]), sb("conv_b", [P, CT])
        dt_b, a_log, dt_w = sb("dt_b", [P, CT]), sb("a_log", [P, CT]), sb("dt_w", [P, CT])
        col_b, col_c, col_d = sb("col_b", [P, CT]), sb("col_c", [P, CT]), sb("col_d", [P, CT])
        exp_a, neg_a = sb("exp_a", [P, CT]), sb("neg_a", [P, CT])
        same_head = sb("same_head", [P, P])
        dt_mat = sb("dt_mat", [P, CT, P])
        conv = sb("conv", [P, 2, SEQ])
        xc, th = sb("xc", [P, CT, SEQ]), sb("th", [P, CT, SEQ])
        soft = sb("soft", [P, 2, SEQ])
        pos = sb("pos", [P, 2, SEQ])
        dt = sb("dt", [P, 2, SEQ])
        decay = sb("decay", [P, 2, SEQ])
        drive = sb("drive", [P, 2, SEQ])
        skip = sb("skip", [P, 2, SEQ])
        state = sb("state", [P, 2, SEQ])
        y = sb("y", [P, TPB, DM])
        pj = [ps(f"pj{i}", [P, SEQ]) for i in range(2)]
        gt = ps("gt", [P, SEQ])
        dtp = [ps(f"dtp{i}", [P, SEQ]) for i in range(2)]
        yo = [ps(f"yo{i}", [P, DM]) for i in range(2)]
        turned = ps("tp", [P, KD, P])
        loaded, cols_loaded = sem("weights_loaded"), sem("columns_loaded")
        head_mask, dt_made, exp_made, neg_made = sem("head_mask"), sem("dt_made"), sem("exp_made"), sem("neg_made")
        pj_ready, gt_ready, dt_ready, yo_ready = sem("pj_ready"), sem("gt_ready"), sem("dt_ready"), sem("yo_ready")
        tap_done = sem("tap_done")
        conv_step = sem("conv_step")
        gt_free = sem("gt_free")
        silu_done = sem("silu_done")
        soft_step = sem("soft_step")
        pos_done = sem("pos_done")
        dt_done = sem("dt_done")
        decay_done = sem("decay_done")
        drive_done = sem("drive_done")
        scan_done = sem("scan_done")
        skip_done = sem("skip_done")
        scaled = sem("scaled")
        gated = sem("gated")
        y_free = sem("y_free")
        block = st.enter_context(nc.Block())

        @block.sync
        def _(e):
            e.dma_start(w_in[:, :, :], io["w_in"]).then_inc(loaded, 16)
            e.dma_start(w_gate[:, :, :], io["w_gate"]).then_inc(loaded, 16)
            for t, name in ((conv_w, "conv_w"), (conv_b, "conv_b"), (dt_b, "dt_b"), (a_log, "a_log"),
                            (dt_w, "dt_w"), (col_b, "col_b"), (col_c, "col_c"), (col_d, "col_d")):
                e.dma_start(t[:], io[name]).then_inc(cols_loaded, 16)
            e.dma_start(w_out[:, :, :], io["w_out"]).then_inc(loaded, 16)
            with e.Fori(0, NB) as b:
                norm_sync(e, n, b, rows(io["x"], b), rows(io["x1"], b))
            e.wait_ge(n.x_stored, 16 * NB + 1)

        @block.gpsimd
        def _(e):
            norm_start(e, n)
            for s, k in ((conv_step, 2 * (TAPS - 1)), (gt_free, 1), (silu_done, 2), (pos_done, 2), (scaled, 2), (y_free, 2)):
                e.sem_inc(s, k)
            e.memset(same_head[:, :], 0.0).then_inc(head_mask, 1)
            e.wait_ge(head_mask, 1)
            e.memset(same_head[0:64, 0:64], 1.0).then_inc(head_mask, 1)
            e.memset(same_head[64:128, 64:128], 1.0).then_inc(head_mask, 1)
            e.wait_ge(head_mask, 3)
            e.wait_ge(cols_loaded, 16 * 8)
            for c in range(CT):
                e.tensor_scalar(dt_mat[:, c, :], same_head[:, :], dt_w[:, c:c + 1], None, ALU.mult).then_inc(dt_made, 1)
            with e.Fori(0, NB) as b:
                for c in range(CT):
                    e.wait_ge(silu_done, b * CT + c + 3)
                    e.wait_ge(scaled, b * CT + c + 1)
                    stand(e, pr.waits_passed)
                    e.tensor_scalar(skip[:, c % 2, :], xc[:, c, :], col_d[:, c:c + 1], None, ALU.mult).then_inc(skip_done, 1)

        @block.tensor
        def _(e):
            e.wait_ge(loaded, 48)
            e.wait_ge(dt_made, CT)
            with e.Fori(0, NB) as b:
                def project(c):
                    e.wait_ge(conv_step, (b * CT + c + 1) * (TAPS - 1))
                    for k in range(KD):
                        mm = e.matmul(pj[c % 2][:, :], w_in[:, k, c * P:(c + 1) * P], XT[:, b, k, :],
                                      start=(k == 0), stop=(k == KD - 1))
                    mm.then_inc(pj_ready, 1)
                    e.wait_ge(gt_free, b * CT + c + 1)
                    for k in range(KD):
                        mm = e.matmul(gt[:, :], w_gate[:, k, c * P:(c + 1) * P], XT[:, b, k, :],
                                      start=(k == 0), stop=(k == KD - 1))
                    mm.then_inc(gt_ready, 1)

                def step_sizes(c):
                    e.wait_ge(silu_done, b * CT + c + 3)
                    e.wait_ge(pos_done, b * CT + c + 1)
                    e.matmul(dtp[c % 2][:, :], dt_mat[:, c, :], xc[:, c, :], start=True, stop=True).then_inc(dt_ready, 1)

                for c in range(5):
                    project(c)
                for c in range(4):
                    step_sizes(c)
                for c in range(5, CT):
                    project(c)
                for c in range(4, CT):
                    step_sizes(c)
                for t in range(TPB):
                    e.wait_ge(y_free, b * TPB + t + 1)
                    for c in range(CT):
                        if t == 0:
                            e.wait_ge(gated, b * CT + c + 1)
                        mm = e.matmul(yo[t % 2][:, :], th[:, c, t * P:(t + 1) * P], w_out[:, c, :],
                                      start=(c == 0), stop=(c == CT - 1))
                    mm.then_inc(yo_ready, 1)
                norm_x_tensor(e, n, b, turned, con["ident"][:, :])

        @block.scalar
        def _(e):
            e.wait_ge(cols_loaded, 16 * 8)
            e.activation(exp_a[:, :], a_log[:, :], ACT.Exp).then_inc(exp_made, 1)
            e.wait_ge(neg_made, 1)
            with e.Fori(0, NB) as b:
                def silu(c):
                    e.wait_ge(conv_step, (b * CT + c + 3) * (TAPS - 1))
                    e.activation(xc[:, c, :], conv[:, c % 2, :], ACT.Silu).then_inc(silu_done, 1)

                def first(c):
                    e.wait_ge(pj_ready, b * CT + c + 1)
                    e.wait_ge(silu_done, b * CT + c + 1)
                    e.activation(conv[:, c % 2, :], pj[c % 2][:, :], ACT.Identity, bias=conv_b[:, c:c + 1],
                                 scale=conv_w[:, c, TAPS - 1:TAPS]).then_inc(tap_done, 1)
                    e.wait_ge(gt_ready, b * CT + c + 1)
                    e.activation(th[:, c, :], gt[:, :], ACT.Tanh, scale=0.5).then_inc(gt_free, 1)

                def step_size(c):
                    z, s = dtp[c % 2][:, :], soft[:, c % 2, :]
                    m = 3 * (b * CT + c)
                    e.wait_ge(dt_ready, b * CT + c + 1)
                    if c >= 2:
                        e.wait_ge(dt_done, b * CT + c - 1)
                    e.activation(s, z, ACT.Abs, bias=dt_b[:, c:c + 1]).then_inc(soft_step, 1)
                    e.activation(pos[:, c % 2, :], z, ACT.Relu, bias=dt_b[:, c:c + 1]).then_inc(pos_done, 1)
                    e.wait_ge(soft_step, m + 1)
                    e.activation(s, s, ACT.Exp, scale=-1.0).then_inc(soft_step, 1)
                    e.wait_ge(soft_step, m + 2)
                    e.activation(s, s, ACT.Ln, bias=1.0).then_inc(soft_step, 1)

                def decays(c):
                    e.wait_ge(dt_done, b * CT + c + 1)
                    if c >= 2:
                        e.wait_ge(scan_done, b * CT + c - 1)
                    e.activation(decay[:, c % 2, :], dt[:, c % 2, :], ACT.Exp, scale=neg_a[:, c:c + 1]).then_inc(decay_done, 1)

                def half(lo, hi):
                    e.preload_act_table_set("natural_log_exp_and_others")
                    for c in range(lo, hi):
                        step_size(c)
                        if c > lo:
                            decays(c - 1)
                    decays(hi - 1)

                first(0)
                for c in range(1, 4):
                    first(c)
                    silu(c - 1)
                silu(3)
                first(4)
                half(0, 4)
                for c in range(5, CT):
                    first(c)
                    silu(c - 1)
                silu(CT - 1)
                half(4, CT)
                for t in range(TPB):
                    e.wait_ge(yo_ready, b * TPB + t + 1)
                    e.activation(y[:, t, :], yo[t % 2][:, :], ACT.Copy, scale=0.5).then_inc(y_free, 1)
                norm_y_scalar(e, n, b, con["eps"][:, :])
                norm_x_scalar(e, n, b, con["eps"][:, :], turned, lambda c: XT[:, b, :, c * P:(c + 1) * P])

        @block.vector
        def _(e):
            e.wait_ge(exp_made, 1)
            e.tensor_scalar(neg_a[:, :], exp_a[:, :], -1.0, None, ALU.mult).then_inc(neg_made, 1)
            with e.Fori(0, NB) as b:
                def taps(c):
                    e.wait_ge(tap_done, b * CT + c + 1)
                    for s in range(1, TAPS):
                        m = (b * CT + c + 2) * (TAPS - 1) + s - 1
                        if s > 1:
                            e.wait_ge(conv_step, m)
                        o = conv[:, c % 2, s:SEQ]
                        e.scalar_tensor_tensor(o, pj[c % 2][:, 0:SEQ - s], conv_w[:, c, TAPS - 1 - s:TAPS - s], o,
                                                     ALU.mult, ALU.add).then_inc(conv_step, 1)

                def scan(c):
                    m, i = b * CT + c, c % 2
                    e.wait_ge(soft_step, 3 * m + 3)
                    e.wait_ge(pos_done, m + 3)
                    e.tensor_tensor(dt[:, i, :], soft[:, i, :], pos[:, i, :], ALU.add).then_inc(dt_done, 1)
                    e.wait_ge(dt_done, m + 1)
                    e.wait_ge(silu_done, m + 3)
                    e.scalar_tensor_tensor(drive[:, i, :], dt[:, i, :], col_b[:, c:c + 1], xc[:, c, :],
                                           ALU.mult, ALU.mult).then_inc(drive_done, 1)
                    e.wait_ge(decay_done, m + 1)
                    e.wait_ge(drive_done, m + 1)
                    e.tensor_tensor_scan(state[:, i, :], decay[:, i, :], drive[:, i, :], 0.0,
                                         ALU.mult, ALU.add).then_inc(scan_done, 1)
                    e.wait_ge(scan_done, m + 1)
                    e.wait_ge(skip_done, m + 1)
                    e.scalar_tensor_tensor(state[:, i, :], state[:, i, :], col_c[:, c:c + 1], skip[:, i, :],
                                           ALU.mult, ALU.add).then_inc(scaled, 1)
                    e.wait_ge(scaled, m + 3)
                    e.wait_ge(gt_free, m + 2)
                    e.scalar_tensor_tensor(th[:, c, :], th[:, c, :], 1.0, state[:, i, :],
                                           ALU.add, ALU.mult).then_inc(gated, 1)

                for c in range(5):
                    taps(c)
                for c in range(4):
                    scan(c)
                for c in range(5, CT):
                    taps(c)
                for c in range(4, CT):
                    scan(c)
                norm_y_vector(e, n, b, lambda c: y[:, c, :], lambda c: e.wait_ge(y_free, b * TPB + c + 3))
                norm_x_vector(e, n, b, lambda c: e.wait_ge(n.x_new, TPB * b + c + 1))


def top2(e, score, shape, t, route, start):
    wide = lambda a: a.unsqueeze(2).to_broadcast(shape)
    prefer = t["prefer"][:, :].unsqueeze(1).to_broadcast(shape)
    n = start

    def after():
        e.wait_ge(route, n)

    rest = score
    for one in ("one1", "one2"):
        after()
        e.tensor_reduce(t["top"][:, :], rest, AX.X, ALU.max).then_inc(route, 1)
        n += 1
        after()
        e.tensor_tensor(t["key"][:, :, :], rest, wide(t["top"][:, :]), ALU.is_equal).then_inc(route, 1)
        n += 1
        after()
        e.tensor_tensor(t["key"][:, :, :], t["key"][:, :, :], prefer, ALU.mult).then_inc(route, 1)
        n += 1
        after()
        e.tensor_reduce(t["top"][:, :], t["key"][:, :, :], AX.X, ALU.max).then_inc(route, 1)
        n += 1
        after()
        e.tensor_tensor(t[one][:, :, :], t["key"][:, :, :], wide(t["top"][:, :]), ALU.is_equal).then_inc(route, 1)
        n += 1
        if one == "one1":
            after()
            e.scalar_tensor_tensor(t["rest"][:, :, :], t["one1"][:, :, :], -2.0, score, ALU.mult, ALU.add).then_inc(route, 1)
            n += 1
            rest = t["rest"][:, :, :]
    return n


def softmax_front(e, logits, t, shape, route, start):
    e.wait_ge(route, start)
    e.tensor_reduce(t["top"][:, :], logits, AX.X, ALU.max).then_inc(route, 1)
    e.wait_ge(route, start + 1)
    e.tensor_tensor(t["score"][:, :, :], logits, t["top"][:, :].unsqueeze(2).to_broadcast(shape), ALU.subtract).then_inc(route, 1)
    return start + 2


def softmax_back(e, t, shape, route, start):
    e.wait_ge(route, start)
    e.tensor_reduce(t["top"][:, :], t["score"][:, :, :], AX.X, ALU.add).then_inc(route, 1)
    e.wait_ge(route, start + 1)
    e.reciprocal(t["inv"][:, :], t["top"][:, :]).then_inc(route, 1)
    e.wait_ge(route, start + 2)
    e.tensor_tensor(t["score"][:, :, :], t["score"][:, :, :], t["inv"][:, :].unsqueeze(2).to_broadcast(shape), ALU.mult).then_inc(route, 1)
    return start + 3


def route_tiles(sb, rows_n):
    t = {k: sb(k, [P, rows_n, NE]) for k in ("score", "key", "rest", "one1", "one2")}
    t["top"], t["inv"] = sb("top", [P, rows_n]), sb("inv", [P, rows_n])
    t["prefer"] = sb("prefer", [P, NE])
    return t


def phase_moe(pr, con, XT):
    nc, io = pr.nc, pr.io
    with ExitStack() as st:
        sb = lambda n, s: pr.sb(st, "b_" + n, s)
        ps = lambda n, s: pr.ps(st, "b_ps_" + n, s)
        sem = lambda n: pr.sem("b_" + n)
        n = Norm(pr, st, "b")
        shape = [P, NT, NE]
        t = route_tiles(sb, NT)
        gate_w = sb("gate_w", [P, KD, NE])
        comb = sb("comb", [P, NT, NX])
        acc = sb("acc", [P, NT, DM])
        w_gu = [sb(f"w_gu{i}", [P, KD, 2 * FE]) for i in range(2)]
        w_dn = [sb(f"w_dn{i}", [P, len(FT), DM]) for i in range(2)]
        hs = [sb(f"hs{i}", [P, SEQ]) for i in range(2)]
        act = sb("act", [P, len(FT), SEQ])
        g_ps = [ps(f"g{i}", [P, SEQ]) for i in range(2)]
        u_ps = [ps(f"u{i}", [P, SEQ]) for i in range(2)]
        y_ps = [ps(f"y{i}", [P, DM]) for i in range(TPB)]
        logits = y_ps[0][:, 0:NT * NE].rearrange("p (t e) -> p t e", e=NE)
        turned = g_ps[0][:, :].rearrange("p (k t) -> p k t", k=KD)
        gate_loaded = sem("gate_loaded")
        w_loaded = [sem("w_loaded0"), sem("w_loaded1")]
        prefer_made, zeroed = sem("prefer_made"), sem("zeroed")
        logits_ready = sem("logits_ready")
        route = sem("route")
        comb_done = sem("comb_done")
        g_ready, u_ready = sem("g_ready"), sem("u_ready")
        silu_done = sem("silu_done")
        act_done = sem("act_done")
        y_ready = sem("y_ready")
        acc_done = sem("acc_done")
        xt_stored = sem("xt_stored")
        block = st.enter_context(nc.Block())

        def load_expert(e, x, par):
            e.dma_start(w_gu[par][:, :, :], io["w_gu"][x]).then_inc(w_loaded[par], 16)
            e.dma_start(w_dn[par][:, 0:2, :], io["w_dn"][x][:, 0:2, :]).then_inc(w_loaded[par], 16)
            e.dma_start(w_dn[par][0:FT[2][1], 2, :], io["w_dn"][x][0:FT[2][1], 2, :]).then_inc(w_loaded[par], 16)

        @block.sync
        def _(e):
            e.dma_start(gate_w[:, :, :], io["gate_w"]).then_inc(gate_loaded, 16)
            for par in range(2):
                load_expert(e, par, par)
            with e.Fori(1, NX // 2) as xp:
                for par in range(2):
                    e.wait_ge(y_ready, (xp * 2 + par - 1) * NT)
                    stand(e, pr.waits_passed)
                    load_expert(e, xp * 2 + par, par)
            with e.Fori(0, NB) as b:
                norm_sync(e, n, b, rows(io["x1"], b), rows(io["x2"], b))
                e.wait_ge(n.xt_done, TPB * b + TPB + 1)
                stand(e, pr.waits_passed)
                e.dma_start(io["xt_d"][b], XT[:, b, :, :]).then_inc(xt_stored, 16)
                e.wait_ge(xt_stored, 16 * b + 16)
                stand(e, pr.waits_passed)
            e.wait_ge(n.x_stored, 16 * NB + 1)

        @block.gpsimd
        def _(e):
            norm_start(e, n)
            for s, k in ((route, 1), (act_done, 3), (acc_done, 4)):
                e.sem_inc(s, k)
            for x in range(NE):
                e.memset(t["prefer"][:, x:x + 1], float(NE - x)).then_inc(prefer_made, 1)
            e.memset(comb[:, :, NE:NX], 1.0).then_inc(zeroed, 1)
            e.memset(acc[:, :, :], 0.0).then_inc(zeroed, 1)

        @block.tensor
        def _(e):
            e.wait_ge(gate_loaded, 16)
            for b in range(NB):
                for c in range(TPB):
                    for k in range(KD):
                        mm = e.matmul(logits[:, b * TPB + c, :], XT[:, b, k, c * P:(c + 1) * P], gate_w[:, k, :],
                                      start=(k == 0), stop=(k == KD - 1))
            mm.then_inc(logits_ready, 1)
            e.wait_ge(route, 3)
            with e.Fori(0, NX // 2) as xp:
                for par in range(2):
                    e.wait_ge(w_loaded[par], 48 * xp + 48)
                    stand(e, pr.waits_passed)
                    with e.Fori(0, NB) as b:
                        u = (xp * 2 + par) * NB + b
                        for f, (lo, width) in enumerate(FT):
                            e.wait_ge(act_done, 3 * u + (3, 3, 4)[f])
                            for dst, at, ready in ((g_ps, lo, g_ready), (u_ps, FE + lo, u_ready)):
                                for k in range(KD):
                                    mm = e.matmul(dst[f % 2][0:width, :], w_gu[par][:, k, at:at + width], XT[:, b, k, :],
                                                  start=(k == 0), stop=(k == KD - 1))
                                mm.then_inc(ready, 1)

                        def down(c, f):
                            return e.matmul(y_ps[c][:, :], act[0:FT[f][1], f, c * P:(c + 1) * P],
                                            w_dn[par][0:FT[f][1], f, :], start=(f == 0), stop=(f == len(FT) - 1))

                        e.wait_ge(act_done, 3 * u + 5)
                        for c in range(TPB):
                            e.wait_ge(acc_done, TPB * u + c + 1)
                            for f in range(2):
                                down(c, f)
                        e.wait_ge(act_done, 3 * u + 6)
                        for c in range(TPB):
                            down(c, 2).then_inc(y_ready, 1)
            with e.Fori(0, NB) as b:
                norm_x_tensor(e, n, b, turned, con["ident"][:, :])

        @block.scalar
        def _(e):
            e.wait_ge(route, 3)
            e.activation(t["score"][:, :, :], t["score"][:, :, :], ACT.Exp).then_inc(route, 1)
            with e.Fori(0, NX // 2) as xp:
                for par in range(2):
                    with e.Fori(0, NB) as b:
                        u = (xp * 2 + par) * NB + b
                        for f, (lo, width) in enumerate(FT):
                            e.wait_ge(g_ready, 3 * u + f + 1)
                            e.activation(hs[f % 2][0:width, :], g_ps[f % 2][0:width, :], ACT.Silu).then_inc(silu_done, 1)
            with e.Fori(0, NB) as b:
                norm_y_scalar(e, n, b, con["eps"][:, :])
                norm_x_scalar(e, n, b, con["eps"][:, :], turned, lambda c: XT[:, b, :, c * P:(c + 1) * P])

        @block.vector
        def _(e):
            e.wait_ge(prefer_made, NE)
            e.wait_ge(logits_ready, 1)
            m = softmax_front(e, logits, t, shape, route, 1)
            m = softmax_back(e, t, shape, route, m + 1)
            m = top2(e, t["score"][:, :, :], shape, t, route, m)
            e.wait_ge(route, m)
            e.tensor_tensor(t["one1"][:, :, :], t["one1"][:, :, :], t["one2"][:, :, :], ALU.add).then_inc(route, 1)
            e.wait_ge(route, m + 1)
            e.wait_ge(zeroed, 2)
            e.tensor_tensor(comb[:, :, 0:NE], t["one1"][:, :, :], t["score"][:, :, :], ALU.mult).then_inc(comb_done, 1)
            e.wait_ge(comb_done, 1)
            with e.Fori(0, NX // 2) as xp:
                for par in range(2):
                    with e.Fori(0, NB) as b:
                        u = (xp * 2 + par) * NB + b
                        for f, (lo, width) in enumerate(FT):
                            e.wait_ge(u_ready, 3 * u + f + 1)
                            e.wait_ge(silu_done, 3 * u + f + 1)
                            e.tensor_tensor(act[0:width, f, :], hs[f % 2][0:width, :], u_ps[f % 2][0:width, :], ALU.mult).then_inc(act_done, 1)
                        for c in range(TPB):
                            e.wait_ge(y_ready, TPB * u + c + 1)
                            tile = acc[:, b * TPB + c, :]
                            weight = comb[:, :, :].unsqueeze(3)[:, b * TPB + c, xp * 2 + par, :]
                            e.scalar_tensor_tensor(tile, y_ps[c][:, :], weight, tile, ALU.mult, ALU.add).then_inc(acc_done, 1)
            with e.Fori(0, NB) as b:
                norm_y_vector(e, n, b, lambda c: acc[:, b * TPB + c, :],
                              lambda c: e.wait_ge(acc_done, NX * NT + 4))
                norm_x_vector(e, n, b, lambda c: e.wait_ge(n.x_new, TPB * b + c + 1))


def gate_tables(pr, stack):
    return {k: pr.sb(stack, k + "_all", [P, NT, NH]) for k in
            ("beta", "log_decay", "decay_before", "decay_upto", "decay_all")}


def phase_gates(pr, con, XT, tab):
    nc, io = pr.nc, pr.io
    with ExitStack() as st:
        sb = lambda n, s: pr.sb(st, "g_" + n, s)
        sem = lambda n: pr.sem("g_" + n)
        w_ab, bias = sb("w_ab", [P, KD, 2 * NH]), sb("bias", [P, 2 * NH])
        z = sb("z", [P, NT, 2 * NH])
        soft = sb("soft", [P, NT, NH])
        z_ps = pr.ps(st, "g_z_ps", [P, NT, 2 * NH])
        cum_ps = [pr.ps(st, f"g_cum{i}", [P, NT, NH]) for i in range(3)]
        loaded, masks, z_ready, z_done = sem("loaded"), sem("masks"), sem("z_ready"), sem("z_done")
        soft_step, la_done, cum_ready = sem("soft_step"), sem("la_done"), sem("cum_ready")
        block = st.enter_context(nc.Block())

        @block.sync
        def _(e):
            e.dma_start(w_ab[:, :, :], io["w_ab"]).then_inc(loaded, 16)
            e.dma_start(bias[:, :], io["b_ab"].partition_broadcast(P)).then_inc(loaded, 16)

        @block.gpsimd
        def _(e):
            for name, base, mul, step in (("before", 0, -1, 1), ("upto", 1, -1, 1), ("after", 0, 1, -1)):
                e.affine_select(out=con[name][:, :], in_=con["ones"][:, :], compare_op=ALU.is_gt, fill=0.0,
                                base=base, pattern=[[step, P]], channel_multiplier=mul).then_inc(masks, 1)

        @block.tensor
        def _(e):
            e.wait_ge(loaded, 32)
            for b in range(NB):
                for c in range(TPB):
                    for k in range(KD):
                        mm = e.matmul(z_ps[:, b * TPB + c, :], XT[:, b, k, c * P:(c + 1) * P], w_ab[:, k, :],
                                      start=(k == 0), stop=(k == KD - 1))
            mm.then_inc(z_ready, 1)
            e.wait_ge(masks, 3)
            e.wait_ge(la_done, 1)
            for dst, mask in zip(cum_ps, ("before", "upto", "ones")):
                e.matmul(dst[:, :, :], con[mask][:, :], tab["log_decay"][:, :, :], start=True, stop=True).then_inc(cum_ready, 1)

        @block.scalar
        def _(e):
            e.wait_ge(z_done, 1)
            e.activation(tab["beta"][:, :, :], z[:, :, NH:2 * NH], ACT.Sigmoid)
            e.preload_act_table_set("natural_log_exp_and_others")
            e.activation(soft[:, :, :], z[:, :, 0:NH], ACT.Abs).then_inc(soft_step, 1)
            e.wait_ge(soft_step, 1)
            e.activation(soft[:, :, :], soft[:, :, :], ACT.Exp, scale=-1.0).then_inc(soft_step, 1)
            e.wait_ge(soft_step, 2)
            e.activation(soft[:, :, :], soft[:, :, :], ACT.Ln, bias=1.0).then_inc(soft_step, 1)
            for i, name in enumerate(("decay_before", "decay_upto", "decay_all")):
                e.wait_ge(cum_ready, i + 1)
                e.activation(tab[name][:, :, :], cum_ps[i][:, :, :], ACT.Exp)

        @block.vector
        def _(e):
            e.wait_ge(z_ready, 1)
            e.wait_ge(loaded, 32)
            e.tensor_tensor(z[:, :, :], z_ps[:, :, :], bias[:, :].unsqueeze(1).to_broadcast([P, NT, 2 * NH]), ALU.add).then_inc(z_done, 1)
            e.wait_ge(z_done, 1)
            e.wait_ge(soft_step, 3)
            e.scalar_tensor_tensor(tab["log_decay"][:, :, :], z[:, :, 0:NH], 0.0, soft[:, :, :], ALU.min, ALU.subtract).then_inc(la_done, 1)


def halves(ap, m):
    v = ap.rearrange("p h (n two m) -> p h n two m", two=2, m=m)
    return v[:, :, :, 0, :], v[:, :, :, 1, :]


def phase_delta(pr, con, tab):
    nc, io = pr.nc, pr.io
    HC = HG * DH
    H4 = [P, HG, P]
    with ExitStack() as st:
        sb = lambda n, s: pr.sb(st, "c_" + n, s)
        ps = lambda n, s: pr.ps(st, "c_ps_" + n, s)
        sem = lambda n: pr.sem("c_" + n)
        w = [sb("w_" + m, [P, KD, HC]) for m in "qkvg"]
        conv_w = [sb(f"conv_w{m}", [P, NH, TAPS]) for m in range(3)]
        conv_b = [sb(f"conv_b{m}", [P, NH]) for m in range(3)]
        ln_w, ln_b = sb("ln_w", [P, DH]), sb("ln_b", [P, DH])
        xs = sb("xs", [P, KD, SEQ])
        qkv = [sb(m + "T", [P, HG, SEQ]) for m in "qkv"]
        qT, kT, vT = qkv
        conv = sb("conv", [P, 2, SEQ])
        gate = sb("gate", [P, TPB, HG, DH])
        beta, log_decay, before, upto, whole = (sb(k, [P, TPB, HG]) for k in ("beta", "log_decay", "before", "upto", "whole"))
        masked_la, masked_b = sb("masked_la", [P, 2, HG, P]), sb("masked_b", [P, 2, HG, P])
        decay = sb("decay", [P, 2, HG, P])
        G = sb("G", [P, 2, HG, P])
        negL = sb("negL", [P, TPB, HG, P])
        A = sb("A", [P, TPB, HG, P])
        R, T = sb("R", [P, TPB, HG, P]), sb("T", [P, TPB, HG, P])
        Z = sb("Z", [P, TPB, HG, P])
        kd = sb("kd", [P, TPB, HG, DH])
        v = sb("v", [P, TPB, HG, DH])
        S = sb("S", [P, HG, DH])
        kS = sb("kS", [P, HG, DH])
        err = sb("err", [P, HG, DH])
        o = sb("o", [P, 2, HG, DH])
        on = sb("on", [P, HG, DH])
        oT = sb("oT", [P, 2, HG, P])
        o_st, o_mv = sb("o_st", [P, HG, 6]), sb("o_mv", [P, HG, 2])
        o_ln, o_rs = sb("o_ln", [P, HG]), sb("o_rs", [P, HG])
        mask_R = [sb(f"mask_R{m}", [P, P // 2]) for m in LEVELS]
        mask_T = [sb(f"mask_T{m}", [P, P // 2]) for m in LEVELS[:-1]]
        pair = sb("pair", [P, P])
        pj = [ps(f"pj{i}", [P, SEQ]) for i in range(2)]
        kk, kq = ps("kk", H4), ps("kq", H4)
        d_ps = ps("d", [P, SEQ])
        z_ps, r_ps, t_ps = (ps(k, [P, SEQ]) for k in ("z", "r", "t"))
        by_head = lambda bank: bank[:, :].rearrange("p (h m) -> p h m", h=HG)
        z4, r4, t4, d4 = by_head(z_ps), by_head(r_ps), by_head(t_ps), by_head(d_ps)
        p4 = [by_head(x) for x in pj]
        half_of = lambda bank: bank[:, 0:HG * P // 2].rearrange("p (h m) -> p h m", h=HG)
        z_half = [half_of(z_ps), half_of(d_ps)]
        r_half = [half_of(r_ps), half_of(pj[1])]
        t_half = [half_of(t_ps), half_of(pj[0])]
        on_heads = lambda a, c: a[:, c, :].unsqueeze(2).to_broadcast(H4)
        over_heads = lambda m: m[:, :].unsqueeze(1).to_broadcast(H4)

        w_loaded, cols_loaded, xs_loaded = sem("w_loaded"), sem("cols_loaded"), sem("xs_loaded")
        masks_made, cleared = sem("masks_made"), sem("cleared")
        tables = sem("tables")
        tables_read = sem("tables_read")
        pj_ready = sem("pj_ready")
        tap_done = sem("tap_done")
        conv_step = sem("conv_step")
        silu_done = sem("silu_done")
        k_scaled = sem("k_scaled")
        g_ready = sem("g_ready")
        g_copied, g_done = sem("g_copied"), sem("g_done")
        la_masked, b_masked = sem("la_masked"), sem("b_masked")
        d_ready, decay_done, G_done = sem("d_ready"), sem("decay_done"), sem("G_done")
        kk_ready, L_done, A_done = sem("kk_ready"), sem("L_done"), sem("A_done")
        R_step = sem("R_step")
        rt_ready, T_done = sem("rt_ready"), sem("T_done")
        kt_ready, kd_done, vt_ready, v_done = sem("kt_ready"), sem("kd_done"), sem("vt_ready"), sem("v_done")
        zl_ready, zl_done = sem("zl_ready"), sem("zl_done")
        rl_ready, rl_done = sem("rl_ready"), sem("rl_done")
        tl_ready, tl_done = sem("tl_ready"), sem("tl_done")
        kS_ready, kS_done, v_less = sem("kS_ready"), sem("kS_done"), sem("v_less")
        qS_ready, qS_done = sem("qS_ready"), sem("qS_done")
        err_ready, err_done = sem("err_ready"), sem("err_done")
        dS_ready, S_decayed, S_done = sem("dS_ready"), sem("S_decayed"), sem("S_done")
        Ae_ready, o_done = sem("Ae_ready"), sem("o_done")
        o_stats, o_mean, o_lned, o_rstd = sem("o_stats"), sem("o_mean"), sem("o_lned"), sem("o_rstd")
        o_normed = sem("o_normed")
        o_gated = sem("o_gated")
        ot_ready = sem("ot_ready")
        ot_done = sem("ot_done")
        ot_stored = [sem("ot_stored0"), sem("ot_stored1")]
        block = st.enter_context(nc.Block())

        @block.sync
        def _(e):
            for m in range(3):
                e.dma_start(conv_w[m][:, :, :], io["conv_w" + "qkv"[m]]).then_inc(cols_loaded, 16)
                e.dma_start(conv_b[m][:, :], io["conv_b" + "qkv"[m]]).then_inc(cols_loaded, 16)
            e.dma_start(ln_w[:, :], io["ln_w"].partition_broadcast(P)).then_inc(cols_loaded, 16)
            e.dma_start(ln_b[:, :], io["ln_b"].partition_broadcast(P)).then_inc(cols_loaded, 16)
            with e.Fori(0, NG) as hg:
                e.wait_ge(g_ready, hg * NB * TPB + TPB)
                stand(e, pr.waits_passed)
                for m in range(4):
                    e.dma_start(w[m][:, :, :], io["w_" + "qkvg"[m]][hg]).then_inc(w_loaded, 16)
                with e.Fori(0, NB) as b:
                    e.wait_ge(g_ready, (hg * NB + b) * TPB + TPB)
                    stand(e, pr.waits_passed)
                    e.dma_start(xs[:, :, :], io["xt_d"][b]).then_inc(xs_loaded, 16)

        @block.gpsimd
        def _(e):
            for s, k in ((tables_read, 1), (conv_step, 2 * (TAPS - 1)), (silu_done, 2), (g_ready, TPB),
                         (ot_done, 1), (ot_stored[0], 16), (ot_stored[1], 16)):
                e.sem_inc(s, k)
            made = 0
            for l, m in enumerate(LEVELS):
                for mask, odd in ((mask_R, 0),) + (((mask_T, 1),) if m < P // 2 else ()):
                    a = mask[l][:, :].rearrange("p (n m) -> p n m", m=m)
                    o1 = con["ones"][:, 0:P // 2].rearrange("p (n m) -> p n m", m=m)
                    lo = odd * m
                    e.affine_select(out=a, in_=o1, compare_op=ALU.is_ge, fill=0.0, base=-lo,
                                    pattern=[[-2 * m, P // 2 // m], [0, m]], channel_multiplier=1).then_inc(masks_made, 1)
                    made += 1
                    e.wait_ge(masks_made, made)
                    e.affine_select(out=a, in_=a, compare_op=ALU.is_gt, fill=0.0, base=lo + m,
                                    pattern=[[2 * m, P // 2 // m], [0, m]], channel_multiplier=-1).then_inc(masks_made, 1)
                    made += 1
            pv = pair[:, :].rearrange("p (n two) -> p n two", two=2)
            ov = con["ones"][:, :].rearrange("p (n two) -> p n two", two=2)
            e.memset(pair[:, :], 0.0).then_inc(masks_made, 1)
            made += 1
            e.wait_ge(masks_made, made)
            e.affine_select(out=pv[:, :, 1], in_=ov[:, :, 1], compare_op=ALU.is_equal, fill=0.0, base=0,
                            pattern=[[-2, P // 2]], channel_multiplier=1).then_inc(masks_made, 1)
            made += 1
            e.wait_ge(masks_made, made)
            for a in (negL, Z):
                e.memset(a[:, :, :, :], 0.0).then_inc(cleared, 1)
            e.wait_ge(cleared, 2)
            e.wait_ge(cols_loaded, 16 * 8)
            with e.Fori(0, NG) as hg, e.Fori(0, NB) as b:
                r = hg * NB + b
                e.wait_ge(tables_read, r + 1)
                stand(e, pr.waits_passed)
                for dst, name in ((beta, "beta"), (log_decay, "log_decay"), (before, "decay_before"),
                                  (upto, "decay_upto"), (whole, "decay_all")):
                    src = tab[name][:, :, :].rearrange("p (b c) (g h) -> p b c g h", c=TPB, h=HG)[:, b, :, hg, :]
                    e.tensor_copy(dst[:, :, :], src).then_inc(tables, 1)
                e.wait_ge(tables, 5 * r + 5)
                stand(e, pr.waits_passed)

                def mask_gates(c):
                    if c >= 2:
                        e.wait_ge(d_ready, r * TPB + c - 1)
                        stand(e, pr.waits_passed)
                    e.tensor_tensor(masked_la[:, c % 2], on_heads(log_decay, c), over_heads(con["upto"]), ALU.mult).then_inc(la_masked, 1)
                    if c >= 2:
                        e.wait_ge(G_done, r * TPB + c - 1)
                        stand(e, pr.waits_passed)
                    e.tensor_tensor(masked_b[:, c % 2], on_heads(beta, c), over_heads(con["upto"]), ALU.mult).then_inc(b_masked, 1)

                for c in range(2):
                    mask_gates(c)
                for h in range(HG):
                    e.wait_ge(silu_done, 12 * r + HG + h + 3)
                    stand(e, pr.waits_passed)
                    e.tensor_scalar(kT[:, h, :], kT[:, h, :], DH ** -0.5, None, ALU.mult).then_inc(k_scaled, 1)
                for c in range(TPB):
                    e.wait_ge(g_copied, r * TPB + c + 1)
                    stand(e, pr.waits_passed)
                    e.tensor_scalar(gate[:, c], gate[:, c], 0.5, 0.5, ALU.mult, ALU.add).then_inc(g_done, 1)
                for c in range(TPB):
                    e.wait_ge(L_done, r * TPB + c + 1)
                    stand(e, pr.waits_passed)
                    e.tensor_tensor(R[:, c], negL[:, c], over_heads(pair), ALU.mult).then_inc(R_step, 1)
                    e.wait_ge(R_step, 2 * (r * TPB + c) + 1)
                    stand(e, pr.waits_passed)
                    e.tensor_tensor(R[:, c], R[:, c], over_heads(con["ident"]), ALU.add).then_inc(R_step, 1)
                    if c + 2 < TPB:
                        mask_gates(c + 2)
                for c in range(TPB):
                    if 0 < c < TPB - 1:
                        e.wait_ge(qS_ready, r * (TPB - 1) + c)
                        e.wait_ge(S_done, r * (TPB - 1) + c)
                        stand(e, pr.waits_passed)
                        e.tensor_tensor(S[:, :, :], S[:, :, :], on_heads(whole, c), ALU.mult).then_inc(S_decayed, 1)
                    e.wait_ge(o_normed, HG * (r * TPB + c + 1))
                    e.wait_ge(g_done, r * TPB + c + 1)
                    stand(e, pr.waits_passed)
                    oc = on[:, :, :]
                    m = 3 * (r * TPB + c)
                    e.tensor_tensor(oc, oc, over_heads(ln_w), ALU.mult).then_inc(o_gated, 1)
                    e.wait_ge(o_gated, m + 1)
                    stand(e, pr.waits_passed)
                    e.tensor_tensor(oc, oc, over_heads(ln_b), ALU.add).then_inc(o_gated, 1)
                    e.wait_ge(o_gated, m + 2)
                    stand(e, pr.waits_passed)
                    e.tensor_tensor(oc, oc, gate[:, c], ALU.mult).then_inc(o_gated, 1)

        @block.tensor
        def _(e):
            with e.Fori(0, NG) as hg:
                e.wait_ge(w_loaded, 64 * hg + 64)
                stand(e, pr.waits_passed)
                with e.Fori(0, NB) as b:
                    r = hg * NB + b
                    chunk = lambda a, h, c: a[:, h, c * P:(c + 1) * P]
                    e.wait_ge(xs_loaded, 16 * r + 16)
                    for u in range(12):
                        e.wait_ge(conv_step, (12 * r + u + 1) * (TAPS - 1))
                        for k in range(KD):
                            mm = e.matmul(pj[u % 2][:, :], w[u // HG][:, k, (u % HG) * DH:(u % HG + 1) * DH], xs[:, k, :],
                                          start=(k == 0), stop=(k == KD - 1))
                        mm.then_inc(pj_ready, 1)
                    for c in range(TPB):
                        if c < 2:
                            e.wait_ge(conv_step, (12 * r + 12 + c + 1) * (TAPS - 1))
                        else:
                            e.wait_ge(g_copied, r * TPB + c - 1)
                        for k in range(KD):
                            mm = e.matmul(pj[c % 2][:, :], xs[:, k, c * P:(c + 1) * P], w[3][:, k, :],
                                          start=(k == 0), stop=(k == KD - 1))
                        mm.then_inc(g_ready, 1)

                    e.wait_ge(silu_done, 12 * r + 14)
                    e.wait_ge(k_scaled, HG * r + HG)
                    for c in range(TPB):
                        n = r * TPB + c
                        e.wait_ge(la_masked, n + 1)
                        if c > 0:
                            e.wait_ge(decay_done, n)
                        else:
                            e.wait_ge(ot_done, n + 1)
                        e.matmul(d4, con["after"][:, :], masked_la[:, c % 2], start=True, stop=True).then_inc(d_ready, 1)
                        if c > 0:
                            e.wait_ge(A_done, n)
                        for h in range(HG):
                            e.matmul(kk[:, h, :], chunk(kT, h, c), chunk(kT, h, c), start=True, stop=True)
                            mm = e.matmul(kq[:, h, :], chunk(kT, h, c), chunk(qT, h, c), start=True, stop=True)
                        mm.then_inc(kk_ready, 1)
                        if c > 0:
                            e.wait_ge(kd_done, n)
                        for h in range(HG):
                            mm = e.transpose(r4[:, h, :], chunk(kT, h, c), con["ident"][:, :])
                        mm.then_inc(kt_ready, 1)
                        if c > 0:
                            e.wait_ge(v_done, n)
                        for h in range(HG):
                            mm = e.transpose(t4[:, h, :], chunk(vT, h, c), con["ident"][:, :])
                        mm.then_inc(vt_ready, 1)
                    for c in range(TPB):
                        n = r * TPB + c
                        e.wait_ge(R_step, 2 * n + 2)
                        if c > 0:
                            e.wait_ge(T_done, n)
                        for h in range(HG):
                            mm = e.transpose(z4[:, h, :], R[:, c, h, :], con["ident"][:, :])
                        mm.then_inc(rt_ready, 1)

                    for l, m in enumerate(LEVELS):
                        for c in range(TPB):
                            i = (r * len(LEVELS) + l) * TPB + c
                            if l == 0:
                                e.wait_ge(T_done, r * TPB + c + 1 if c >= 2 else r * TPB + TPB)
                            else:
                                e.wait_ge(tl_done, (r * (len(LEVELS) - 1) + l - 1) * TPB + c + 1)
                            if c >= 2 or l > 0:
                                e.wait_ge(zl_done, i - 1)
                            even, _odd = halves(T[:, c], m)
                            for h in range(HG):
                                mm = e.matmul(z_half[c % 2][:, h, :], negL[:, c, h, :], even[:, h], start=True, stop=True)
                            mm.then_inc(zl_ready, 1)
                        for c in range(TPB):
                            i = (r * len(LEVELS) + l) * TPB + c
                            e.wait_ge(zl_done, i + 1)
                            if l == 0 and c < 2:
                                e.wait_ge(kd_done, r * TPB + TPB)
                                e.wait_ge(v_done, r * TPB + TPB)
                                e.wait_ge(g_copied, r * TPB + TPB)
                            else:
                                e.wait_ge(rl_done, i - 1)
                            even, _odd = halves(Z[:, c], m)
                            _even, odd = halves(R[:, c], m)
                            for h in range(HG):
                                mm = e.matmul(r_half[c % 2][:, h, :], Z[:, c, h, :], odd[:, h], start=True, stop=True)
                            mm.then_inc(rl_ready, 1)
                            if m < P // 2:
                                j = (r * (len(LEVELS) - 1) + l) * TPB + c
                                if not (l == 0 and c < 2):
                                    e.wait_ge(tl_done, j - 1)
                                for h in range(HG):
                                    mm = e.matmul(t_half[c % 2][:, h, :], R[:, c, h, :], even[:, h], start=True, stop=True)
                                mm.then_inc(tl_ready, 1)

                    def turn_out(c):
                        n = r * TPB + c
                        e.wait_ge(o_gated, 3 * n + 3)
                        if c > 0:
                            e.wait_ge(ot_done, n + 1)
                        else:
                            e.wait_ge(decay_done, r * TPB + TPB)
                        for h in range(HG):
                            mm = e.transpose(d4[:, h, :], on[:, h, :], con["ident"][:, :])
                        mm.then_inc(ot_ready, 1)

                    for c in range(TPB):
                        n, m = r * TPB + c, r * (TPB - 1) + c
                        if c > 0:
                            e.wait_ge(S_done, m)
                            if c == 1:
                                e.wait_ge(rl_done, (r + 1) * len(LEVELS) * TPB)
                            else:
                                e.wait_ge(kS_done, m - 1)
                                e.wait_ge(qS_done, m - 1)
                            for h in range(HG):
                                mm = e.matmul(p4[0][:, h, :], chunk(kT, h, c), S[:, h, :], start=True, stop=True)
                            mm.then_inc(kS_ready, 1)
                            for h in range(HG):
                                mm = e.matmul(p4[1][:, h, :], chunk(qT, h, c), S[:, h, :], start=True, stop=True)
                            mm.then_inc(qS_ready, 1)
                            e.wait_ge(v_less, m)
                        e.wait_ge(rl_done, (r * len(LEVELS) + len(LEVELS) - 1) * TPB + c + 1)
                        if c > 0:
                            e.wait_ge(err_done, n)
                        for h in range(HG):
                            mm = e.matmul(z4[:, h, :], R[:, c, h, :], v[:, c, h, :], start=True, stop=True)
                        mm.then_inc(err_ready, 1)
                        e.wait_ge(err_done, n + 1)
                        if c < TPB - 1:
                            for h in range(HG):
                                mm = e.matmul(kq[:, h, :], kd[:, c, h, :], err[:, h, :], start=True, stop=True)
                            mm.then_inc(dS_ready, 1)
                        if c > 0:
                            e.wait_ge(o_done, n)
                        for h in range(HG):
                            mm = e.matmul(kk[:, h, :], A[:, c, h, :], err[:, h, :], start=True, stop=True)
                        mm.then_inc(Ae_ready, 1)
                        if c > 0:
                            turn_out(c - 1)
                    turn_out(TPB - 1)

        @block.scalar
        def _(e):
            e.wait_ge(cols_loaded, 16 * 8)
            with e.Fori(0, NG) as hg, e.Fori(0, NB) as b:
                r = hg * NB + b

                def silu(u):
                    e.wait_ge(conv_step, (12 * r + u + 3) * (TAPS - 1))
                    e.activation(qkv[u // HG][:, u % HG, :], conv[:, u % 2, :], ACT.Silu).then_inc(silu_done, 1)

                e.preload_act_table_set("silu_and_others")
                for u in range(12):
                    cw, cb = conv_w[u // HG][:, :, :], conv_b[u // HG][:, :].unsqueeze(2)
                    e.wait_ge(pj_ready, 12 * r + u + 1)
                    e.wait_ge(silu_done, 12 * r + u + 1)
                    e.activation(conv[:, u % 2, :], pj[u % 2][:, :], ACT.Identity, bias=cb[:, hg * HG + u % HG, :],
                                 scale=cw[:, hg * HG + u % HG, TAPS - 1:TAPS]).then_inc(tap_done, 1)
                    if u > 0:
                        silu(u - 1)
                silu(11)
                for c in range(TPB):
                    e.wait_ge(g_ready, r * TPB + c + TPB + 1)
                    e.activation(gate[:, c], p4[c % 2], ACT.Tanh, scale=0.5).then_inc(g_copied, 1)
                e.preload_act_table_set("natural_log_exp_and_others")
                for c in range(TPB):
                    n = r * TPB + c
                    e.wait_ge(d_ready, n + 1)
                    if c >= 2:
                        e.wait_ge(G_done, n - 1)
                    e.activation(decay[:, c % 2], d4, ACT.Exp).then_inc(decay_done, 1)
                    e.wait_ge(vt_ready, n + 1)
                    e.activation(v[:, c], t4, ACT.Copy).then_inc(v_done, 1)
                for c in range(TPB):
                    e.wait_ge(rt_ready, r * TPB + c + 1)
                    e.activation(T[:, c], z4, ACT.Copy).then_inc(T_done, 1)
                for l, m in enumerate(LEVELS):
                    for c in range(TPB):
                        i = (r * len(LEVELS) + l) * TPB + c
                        e.wait_ge(zl_ready, i + 1)
                        even, _odd = halves(Z[:, c], m)
                        e.activation(even, z_half[c % 2].rearrange("p h (n m) -> p h n m", m=m), ACT.Copy).then_inc(zl_done, 1)

                def rstd(c):
                    n = r * TPB + c
                    e.wait_ge(o_mean, HG * (n + 1))
                    e.activation(o_ln[:, :], o_mv[:, :, 1], ACT.Ln, bias=con["eps"][:, :]).then_inc(o_lned, 1)
                    e.wait_ge(o_lned, n + 1)
                    e.activation(o_rs[:, :], o_ln[:, :], ACT.Exp, scale=-0.5).then_inc(o_rstd, 1)

                def store(c):
                    n = r * TPB + c
                    e.wait_ge(ot_ready, n + 1)
                    e.wait_ge(ot_stored[c % 2], 16 * (r * 2 + c // 2) + 16)
                    e.activation(oT[:, c % 2], d4, ACT.Copy).then_inc(ot_done, 1)
                    e.wait_ge(ot_done, n + 2)
                    stand(e, pr.waits_passed)
                    dst = io["ot_d"].rearrange("t p (g h) m -> t p g h m", h=HG)[b * TPB + c, :, hg, :, :]
                    e.dma_start(dst, oT[:, c % 2]).then_inc(ot_stored[c % 2], 16)

                for c in range(TPB):
                    n = r * TPB + c
                    e.wait_ge(err_ready, n + 1)
                    e.activation(err[:, :, :], z4, ACT.Copy).then_inc(err_done, 1)
                    rstd(c)
                    if c > 0:
                        store(c - 1)
                store(TPB - 1)
            for s in ot_stored:
                e.wait_ge(s, 16 * NB * NG * 2 + 16)

        @block.vector
        def _(e):
            e.wait_ge(cols_loaded, 16 * 8)
            e.wait_ge(cleared, 2)
            with e.Fori(0, NG) as hg, e.Fori(0, NB) as b:
                r = hg * NB + b
                for u in range(12):
                    cw = conv_w[u // HG][:, :, :]
                    e.wait_ge(tap_done, 12 * r + u + 1)
                    for s in range(1, TAPS):
                        if s > 1:
                            e.wait_ge(conv_step, (12 * r + u + 2) * (TAPS - 1) + s - 1)
                        oc = conv[:, u % 2, s:SEQ]
                        e.scalar_tensor_tensor(oc, pj[u % 2][:, 0:SEQ - s], cw[:, hg * HG + u % HG, TAPS - 1 - s:TAPS - s], oc,
                                               ALU.mult, ALU.add).then_inc(conv_step, 1)
                for c in range(TPB):
                    n = r * TPB + c
                    e.wait_ge(decay_done, n + 1)
                    e.wait_ge(b_masked, n + 1)
                    e.tensor_tensor(G[:, c % 2], decay[:, c % 2], masked_b[:, c % 2], ALU.mult).then_inc(G_done, 1)
                    e.wait_ge(G_done, n + 1)
                    e.wait_ge(kk_ready, n + 1)
                    e.scalar_tensor_tensor(negL[:, c, :, 1:P], kk[:, :, 1:P], -1.0, G[:, c % 2, :, 0:P - 1],
                                           ALU.mult, ALU.mult).then_inc(L_done, 1)
                    e.tensor_tensor(A[:, c], kq[:, :, :], G[:, c % 2], ALU.mult).then_inc(A_done, 1)
                    e.wait_ge(kt_ready, n + 1)
                    e.tensor_tensor(kd[:, c], r4, G[:, c % 2, :, P - 1:P].to_broadcast(H4), ALU.mult).then_inc(kd_done, 1)
                for l, m in enumerate(LEVELS):
                    for c in range(TPB):
                        i = (r * len(LEVELS) + l) * TPB + c
                        j = (r * (len(LEVELS) - 1) + l) * TPB + c
                        as_blocks = lambda a: a.rearrange("p h (n m) -> p h n m", m=m)
                        wide = lambda a: a[:, :].bitcast(U32).rearrange("p (n m) -> p n m", m=m).unsqueeze(1).to_broadcast([P, HG, P // 2 // m, m])
                        e.wait_ge(rl_ready, i + 1)
                        if m < P // 2:
                            e.wait_ge(tl_ready, j + 1)
                        stand(e, pr.waits_passed)
                        _even, odd = halves(R[:, c], m)
                        e.copy_predicated(odd, wide(mask_R[l]), as_blocks(r_half[c % 2])).then_inc(rl_done, 1)
                        if m < P // 2:
                            even, _odd = halves(T[:, c], m)
                            e.copy_predicated(even, wide(mask_T[l]), as_blocks(t_half[c % 2])).then_inc(tl_done, 1)
                for c in range(TPB):
                    n, m = r * TPB + c, r * (TPB - 1) + c
                    oc = o[:, c % 2]
                    if c > 0:
                        e.wait_ge(kS_ready, m)
                        e.tensor_tensor(kS[:, :, :], p4[0], on_heads(before, c), ALU.mult).then_inc(kS_done, 1)
                        e.wait_ge(kS_done, m)
                        e.wait_ge(v_done, n + 1)
                        e.tensor_tensor(v[:, c], v[:, c], kS[:, :, :], ALU.subtract).then_inc(v_less, 1)
                        e.wait_ge(qS_ready, m)
                        e.tensor_tensor(oc, p4[1], on_heads(upto, c), ALU.mult).then_inc(qS_done, 1)
                    if c < TPB - 1:
                        e.wait_ge(dS_ready, m + 1)
                        if c == 0:
                            e.tensor_copy(S[:, :, :], kq[:, :, :]).then_inc(S_done, 1)
                        else:
                            e.wait_ge(S_decayed, r * (TPB - 2) + c)
                            e.tensor_tensor(S[:, :, :], S[:, :, :], kq[:, :, :], ALU.add).then_inc(S_done, 1)
                    e.wait_ge(Ae_ready, n + 1)
                    if c == 0:
                        e.tensor_copy(oc, kk[:, :, :]).then_inc(o_done, 1)
                    else:
                        e.wait_ge(qS_done, m)
                        e.tensor_tensor(oc, oc, kk[:, :, :], ALU.add).then_inc(o_done, 1)
                    e.wait_ge(o_done, n + 1)
                    for h in range(HG):
                        e.bn_stats(o_st[:, h, :], o[:, c % 2, h, :]).then_inc(o_stats, 1)
                    e.wait_ge(o_stats, HG * (n + 1))
                    stand(e, pr.waits_passed)
                    for h in range(HG):
                        e.bn_aggr(o_mv[:, h, :], o_st[:, h, :]).then_inc(o_mean, 1)
                    e.wait_ge(o_rstd, n + 1)
                    if c > 0:
                        e.wait_ge(ot_ready, n)
                    for h in range(HG):
                        e.tensor_scalar(on[:, h, :], o[:, c % 2, h, :], o_mv[:, h, 0:1], o_rs[:, h:h + 1],
                                        ALU.subtract, ALU.mult).then_inc(o_normed, 1)
                e.wait_ge(o_normed, HG * (r * TPB + TPB))
                e.sem_inc(tables_read, 1)


def phase_delta_out(pr, con, XT, route_part):
    nc, io = pr.nc, pr.io
    with ExitStack() as st:
        sb = lambda n, s: pr.sb(st, "d_" + n, s)
        ps = lambda n, s: pr.ps(st, "d_ps_" + n, s)
        sem = lambda n: pr.sem("d_" + n)
        n = Norm(pr, st, "d")
        w_o = sb("w_o", [P, NH, DM])
        heads = sb("heads", [P, TPB, NH, P])
        switch = sb("switch", [P, NE, TPB * DM])
        products = sb("products", [P, TPB * DM])
        part = sb("part", [P, NE])
        y = sb("y", [P, TPB, DM])
        yo = [ps(f"yo{i}", [P, DM]) for i in range(2)]
        turned = ps("tp", [P, KD, P])
        wo_loaded, switch_loaded = sem("wo_loaded"), sem("switch_loaded")
        heads_loaded = [sem(f"heads_loaded{c}") for c in range(TPB)]
        yo_ready = sem("yo_ready")
        y_free = sem("y_free")
        switched = sem("switched")
        part_kept = sem("part_kept")
        block = st.enter_context(nc.Block())

        @block.sync
        def _(e):
            e.dma_start(w_o[:, :, :], io["w_o"]).then_inc(wo_loaded, 16)
            with e.Fori(0, NB) as b:
                for c in range(TPB):
                    e.wait_ge(yo_ready, b * TPB + c + 1)
                    stand(e, pr.waits_passed)
                    e.dma_start(heads[:, c, :, :], io["ot_d"][b * TPB + c]).then_inc(heads_loaded[c], 16)
                norm_sync(e, n, b, rows(io["x2"], b), rows(io["x3"], b))
            e.wait_ge(n.x_stored, 16 * NB + 1)

        @block.gpsimd
        def _(e):
            norm_start(e, n)
            for s, k in ((yo_ready, TPB), (y_free, 2), (switched, 1), (part_kept, 1)):
                e.sem_inc(s, k)
            e.dma_start(switch[:, :, :], io["switch_w"]).then_inc(switch_loaded, 16)

        @block.tensor
        def _(e):
            e.wait_ge(wo_loaded, 16)
            with e.Fori(0, NB) as b:
                for c in range(TPB):
                    e.wait_ge(heads_loaded[c], 16 * b + 16)
                    e.wait_ge(y_free, b * TPB + c + 1)
                    for h in range(NH):
                        mm = e.matmul(yo[c % 2][:, :], heads[:, c, h, :], w_o[:, h, :], start=(h == 0), stop=(h == NH - 1))
                    mm.then_inc(yo_ready, 1)
                norm_x_tensor(e, n, b, turned, con["ident"][:, :])

        @block.scalar
        def _(e):
            with e.Fori(0, NB) as b:
                for c in range(TPB):
                    e.wait_ge(yo_ready, b * TPB + c + TPB + 1)
                    e.activation(y[:, c, :], yo[c % 2][:, :], ACT.Copy).then_inc(y_free, 1)
                norm_y_scalar(e, n, b, con["eps"][:, :])
                norm_x_scalar(e, n, b, con["eps"][:, :], turned, lambda c: XT[:, b, :, c * P:(c + 1) * P])

        @block.vector
        def _(e):
            with e.Fori(0, NB) as b:
                norm_y_vector(e, n, b, lambda c: y[:, c, :], lambda c: e.wait_ge(y_free, b * TPB + c + 3))
                norm_x_vector(e, n, b, lambda c: e.wait_ge(n.x_new, TPB * b + c + 1))
                e.wait_ge(switch_loaded, 16)
                e.wait_ge(n.x_normed, TPB * b + TPB + 1)
                e.wait_ge(part_kept, b + 1)
                for x in range(NE):
                    e.wait_ge(switched, NE * b + x + 1)
                    e.scalar_tensor_tensor(products[:, :], n.yn[:, :, :].rearrange("p c d -> p (c d)"), 1.0, switch[:, x, :],
                                           ALU.mult, ALU.mult, accum_out=part[:, x:x + 1]).then_inc(switched, 1)
                e.wait_ge(switched, NE * b + NE + 1)
                e.tensor_copy(route_part[:, b, :], part[:, :]).then_inc(part_kept, 1)


def phase_experts(pr, con, XT, route_part):
    nc, io = pr.nc, pr.io
    HB = P // FH
    with ExitStack() as st:
        sb = lambda n, s: pr.sb(st, "e_" + n, s)
        ps = lambda n, s: pr.ps(st, "e_ps_" + n, s)
        sem = lambda n: pr.sem("e_" + n)
        n = Norm(pr, st, "e")
        shape = [P, NB, NE]
        t = route_tiles(lambda k, s: sb("r_" + k, s), NB)
        switch_b = sb("switch_b", [P, NE])
        w1, w2 = sb("w1", [P, FH, NE]), sb("w2", [P, FH, NE])
        b1, b2 = sb("b1", [P, NE]), sb("b2", [P, NE])
        w3, b3 = sb("w3", [P, KD, DM]), sb("b3", [P, DM])
        chosen = [sb(f"chosen{i}", [P, FH, NE]) for i in range(2)]
        w1_sel, w2_sel = sb("w1_sel", [P, NB, 2, FH]), sb("w2_sel", [P, NB, 2, FH])
        b1_sel, b2_sel = sb("b1_sel", [P, NB, 2]), sb("b2_sel", [P, NB])
        same_head = sb("same_head", [P, P])
        w1_diag, w2_diag = sb("w1_diag", [P, 2, HB, FH]), sb("w2_diag", [P, 2, HB, FH])
        hidden = sb("hidden", [P, 2, 2, SEQ])
        mixed = sb("mixed", [P, KD, SEQ])
        y = sb("y", [P, TPB, DM])
        l_ps = ps("logits", [P, NB, NE])
        h_ps = [ps(f"h{i}", [P, SEQ]) for i in range(2)]
        o_ps = [ps(f"o{i}", [P, SEQ]) for i in range(2)]
        y_ps = [ps(f"y{i}", [P, DM]) for i in range(2)]
        loaded = sem("loaded")
        masks = sem("masks")
        route = sem("route")
        logits_ready = sem("logits_ready")
        diag_done = sem("diag_done")
        h_ready = sem("h_ready")
        gelu_done = sem("gelu_done")
        o_ready = sem("o_ready")
        mixed_done = sem("mixed_done")
        y_ready, y_done = sem("y_ready"), sem("y_done")
        block = st.enter_context(nc.Block())

        @block.sync
        def _(e):
            for dst, name in ((w1, "w1"), (w2, "w2"), (b1, "b1"), (b2, "b2"), (w3, "w3")):
                e.dma_start(dst[:], io[name]).then_inc(loaded, 16)
            e.dma_start(switch_b[:, :], io["switch_b"].partition_broadcast(P)).then_inc(loaded, 16)
            e.dma_start(b3[:, :], io["b3"].partition_broadcast(P)).then_inc(loaded, 16)
            with e.Fori(0, NB) as b:
                norm_sync(e, n, b, rows(io["x3"], b), rows(io["out"], b))
            e.wait_ge(n.x_stored, 16 * NB + 1)

        @block.gpsimd
        def _(e):
            norm_start(e, n)
            e.sem_inc(n.x_normed, NB * TPB)
            e.sem_inc(n.turned, NB * TPB)
            for s, k in ((route, 1), (gelu_done, 2), (mixed_done, 2), (y_done, 2)):
                e.sem_inc(s, k)
            for x in range(NE):
                e.memset(t["prefer"][:, x:x + 1], float(NE - x)).then_inc(masks, 1)
            e.memset(same_head[:, :], 0.0).then_inc(masks, 1)
            e.wait_ge(masks, NE + 1)
            for j in range(HB):
                e.memset(same_head[j * FH:(j + 1) * FH, j * FH:(j + 1) * FH], 1.0).then_inc(masks, 1)

        @block.tensor
        def _(e):
            e.matmul(l_ps[:, :, :], con["ones"][:, :], route_part[:, :, :], start=True, stop=True).then_inc(logits_ready, 1)
            e.wait_ge(loaded, 16 * 7)
            with e.Fori(0, NB) as b:
                def hidden_layer(dc):
                    for k in range(2):
                        e.wait_ge(gelu_done, 8 * b + 2 * dc + k + 1)
                        e.matmul(h_ps[k][:, :], w1_diag[:, k].rearrange("p j f -> p (j f)"), XT[:, b, dc, :],
                                 start=True, stop=True).then_inc(h_ready, 1)

                def output_layer(dc):
                    e.wait_ge(mixed_done, KD * b + dc + 1)
                    for k in range(2):
                        e.wait_ge(gelu_done, 8 * b + 2 * dc + k + 3)
                        mm = e.matmul(o_ps[dc % 2][:, :], w2_diag[:, k].rearrange("p j f -> p (j f)"), hidden[:, dc % 2, k, :],
                                      start=(k == 0), stop=(k == 1))
                    mm.then_inc(o_ready, 1)

                e.wait_ge(diag_done, 4 * b + 4)
                hidden_layer(0)
                for dc in range(1, KD):
                    hidden_layer(dc)
                    output_layer(dc - 1)
                output_layer(KD - 1)
                e.wait_ge(mixed_done, KD * b + KD + 2)
                for c in range(TPB):
                    e.wait_ge(y_done, TPB * b + c + 1)
                    for k in range(KD):
                        mm = e.matmul(y_ps[c % 2][:, :], mixed[:, k, c * P:(c + 1) * P], w3[:, k, :],
                                      start=(k == 0), stop=(k == KD - 1))
                    mm.then_inc(y_ready, 1)

        @block.scalar
        def _(e):
            e.wait_ge(route, 4)
            e.activation(t["score"][:, :, :], t["score"][:, :, :], ACT.Exp).then_inc(route, 1)
            with e.Fori(0, NB) as b:
                for dc in range(KD):
                    for k in range(2):
                        e.wait_ge(h_ready, 8 * b + 2 * dc + k + 1)
                        stand(e, pr.waits_passed)
                        e.activation(hidden[:, dc % 2, k, :], h_ps[k][:, :], ACT.Gelu,
                                     bias=b1_sel[:, :, :].unsqueeze(3)[:, b, k, :]).then_inc(gelu_done, 1)
                norm_y_scalar(e, n, b, con["eps"][:, :])

        @block.vector
        def _(e):
            e.wait_ge(loaded, 16 * 7)
            e.wait_ge(masks, NE + 1 + HB)
            e.wait_ge(logits_ready, 1)
            e.tensor_tensor(t["rest"][:, :, :], l_ps[:, :, :], switch_b[:, :].unsqueeze(1).to_broadcast(shape), ALU.add).then_inc(route, 1)
            m = softmax_front(e, t["rest"][:, :, :], t, shape, route, 2)
            m = softmax_back(e, t, shape, route, m + 1)
            m = top2(e, t["score"][:, :, :], shape, t, route, m)
            e.wait_ge(route, m)
            for one, gated in (("one1", "key"), ("one2", "rest")):
                e.tensor_tensor(t[gated][:, :, :], t[one][:, :, :], t["score"][:, :, :], ALU.mult).then_inc(route, 1)
            m += 2
            e.wait_ge(route, m)

            def choose(dst, table, row, step):
                i = step % 2
                e.wait_ge(route, step)
                e.tensor_tensor(chosen[i][:, :, :], table[:, :, :], row.unsqueeze(1).to_broadcast([P, FH, NE]), ALU.mult).then_inc(route, 1)
                e.wait_ge(route, step + 1)
                e.tensor_reduce(dst, chosen[i][:, :, :], AX.X, ALU.add).then_inc(route, 1)
                return step + 2

            def choose_bias(dst, table, row, step):
                e.wait_ge(route, step)
                e.tensor_tensor(chosen[0][:, 0, :], table[:, :], row, ALU.mult).then_inc(route, 1)
                e.wait_ge(route, step + 1)
                e.tensor_reduce(dst, chosen[0][:, 0, :], AX.X, ALU.add).then_inc(route, 1)
                return step + 2

            for b in range(NB):
                for k, (one, gated) in enumerate((("one1", "key"), ("one2", "rest"))):
                    m = choose(w1_sel[:, b, k, :], w1, t[one][:, b, :], m)
                    m = choose(w2_sel[:, b, k, :], w2, t[gated][:, b, :], m)
                    m = choose_bias(b1_sel[:, b, k:k + 1], b1, t[one][:, b, :], m)
                e.wait_ge(route, m)
                e.tensor_tensor(t["score"][:, b, :], t["key"][:, b, :], t["rest"][:, b, :], ALU.add).then_inc(route, 1)
                m = choose_bias(b2_sel[:, b:b + 1], b2, t["score"][:, b, :], m + 1)
            e.wait_ge(route, m)
            heads4 = same_head[:, :].rearrange("p (j f) -> p j f", j=HB)
            with e.Fori(0, NB) as b:
                for sel, diag in ((w1_sel, w1_diag), (w2_sel, w2_diag)):
                    for k in range(2):
                        e.tensor_tensor(diag[:, k], heads4, sel[:, b, k, :].unsqueeze(1).to_broadcast([P, HB, FH]), ALU.mult).then_inc(diag_done, 1)
                for dc in range(KD):
                    e.wait_ge(o_ready, KD * b + dc + 1)
                    e.scalar_tensor_tensor(mixed[:, dc, :], o_ps[dc % 2][:, :], b2_sel[:, :].unsqueeze(2)[:, b, :], XT[:, b, dc, :],
                                           ALU.add, ALU.add).then_inc(mixed_done, 1)
                for c in range(TPB):
                    e.wait_ge(y_ready, TPB * b + c + 1)
                    e.tensor_tensor(y[:, c, :], y_ps[c % 2][:, :], b3[:, :], ALU.add).then_inc(y_done, 1)
                norm_y_vector(e, n, b, lambda c: y[:, c, :], lambda c: e.wait_ge(y_done, TPB * b + c + 3))


def program(nc, io):
    for name in ("x1", "x2", "x3"):
        io[name] = nc.dram_tensor(name, [NB, SEQ, DM], F32).ap()
    io["xt_d"] = nc.dram_tensor("xt_d", [NB, P, KD, SEQ], F32).ap()
    io["ot_d"] = nc.dram_tensor("ot_d", [NT, P, NH, P], F32).ap()
    pr = Program(nc, io)
    with pr.lasting as lasting:
        con = constants(pr, lasting)
        with ExitStack() as first:
            tab = gate_tables(pr, first)
            with ExitStack() as st:
                XT = pr.sb(st, "XT", [P, NB, KD, SEQ])
                phase_first_norm(pr, con, XT)
                phase_ssm(pr, con, XT)
                pr.retire_sems()
                phase_moe(pr, con, XT)
                phase_gates(pr, con, XT, tab)
            phase_delta(pr, con, tab)
        pr.retire_sems()
        XT = pr.sb(lasting, "XT2", [P, NB, KD, SEQ])
        route_part = pr.sb(lasting, "route_part", [P, NB, NE])
        phase_delta_out(pr, con, XT, route_part)
        phase_experts(pr, con, XT, route_part)


def host_layout(d):
    import numpy as np
    col = lambda a: np.ascontiguousarray(np.asarray(a).reshape(CT, P).T)
    chunks = lambda a: np.ascontiguousarray(np.asarray(a).reshape(-1, P, np.shape(a)[-1]).transpose(1, 0, 2))
    g = {k: np.asarray(v) for k, v in d.items()}
    o = {}
    o["x"] = g["L0_attn_hidden_states"]
    o["w_in"] = chunks(g["L0_attn_in_proj_w"].T)
    o["w_gate"] = chunks(g["L0_attn_gate_proj_w"].T)
    o["w_out"] = chunks(g["L0_attn_out_proj_w"].T)
    o["conv_w"] = np.ascontiguousarray(g["L0_attn_conv_weight"].reshape(CT, P, TAPS).transpose(1, 0, 2))
    o["conv_b"] = col(g["L0_attn_conv_bias"])
    o["dt_w"] = col(g["L0_attn_dt_w"])
    o["dt_b"] = col(np.repeat(g["L0_attn_dt_b"], 64))
    o["a_log"] = col(g["L0_attn_A_log"])
    o["col_b"], o["col_c"], o["col_d"] = col(g["L0_attn_B"]), col(g["L0_attn_C"]), col(g["L0_attn_D"])
    sgu, sdn = g["L0_ffn_shared_gate_up"], g["L0_ffn_shared_down"]
    fs = NSH * FE
    gu = np.concatenate([g["L0_ffn_gate_up_weights"]] + [
        np.concatenate([sgu[i * FE:(i + 1) * FE], sgu[fs + i * FE:fs + (i + 1) * FE]])[None] for i in range(NSH)])
    o["w_gu"] = np.ascontiguousarray(gu.transpose(0, 2, 1).reshape(NX, KD, P, 2 * FE).transpose(0, 2, 1, 3))
    dn = np.concatenate([g["L0_ffn_down_weights"]] + [sdn[None, :, i * FE:(i + 1) * FE] for i in range(NSH)])
    rows_in = np.zeros((NX, len(FT) * P, DM), dn.dtype)
    rows_in[:, :FE] = dn.transpose(0, 2, 1)
    o["w_dn"] = np.ascontiguousarray(rows_in.reshape(NX, len(FT), P, DM).transpose(0, 2, 1, 3))
    o["gate_w"] = chunks(g["L0_ffn_gate_weight"].T)
    for m in "qkvg":
        wm = g["L1_attn_W" + m].reshape(KD, P, NG, HG * DH)
        o["w_" + m] = np.ascontiguousarray(wm.transpose(2, 1, 0, 3))
    for m in "qkv":
        o["conv_w" + m] = np.ascontiguousarray(g[f"L1_attn_{m}cw"].reshape(NH, DH, TAPS).transpose(1, 0, 2))
        o["conv_b" + m] = np.ascontiguousarray(g[f"L1_attn_{m}cb"].reshape(NH, DH).T)
    o["w_ab"] = chunks(np.concatenate([g["L1_attn_Wa"], g["L1_attn_Wb"]], 1))
    o["b_ab"] = np.concatenate([g["L1_attn_ba"], g["L1_attn_bb"]])
    o["ln_w"], o["ln_b"] = g["L1_attn_ln_w"], g["L1_attn_ln_b"]
    o["w_o"] = chunks(g["L1_attn_Wo"])
    o["switch_w"] = np.ascontiguousarray(g["L1_ffn_switch_w"].reshape(NE, TPB, P, DM).transpose(2, 0, 1, 3).reshape(P, NE, TPB * DM))
    o["switch_b"], o["b3"] = g["L1_ffn_switch_b"], g["L1_ffn_b3"]
    per_head = lambda a: np.ascontiguousarray(np.tile(a, (P // FH,) + (1,) * (a.ndim - 1)))
    o["w1"], o["w2"] = per_head(g["L1_ffn_w1"].transpose(2, 1, 0)), per_head(g["L1_ffn_w2"].transpose(2, 1, 0))
    o["b1"], o["b2"] = per_head(g["L1_ffn_b1"].T), per_head(g["L1_ffn_b2"].T)
    o["w3"] = chunks(g["L1_ffn_w3"].T)
    return o


def kernel(**inputs):
    import numpy as np
    import concourse.bacc as bacc
    from concourse.bass_utils import run_bass_kernel_spmd

    nc = bacc.Bacc("TRN2", target_bir_lowering=False, num_devices=1)
    arrays, io = {}, {}
    for name, a in host_layout(inputs).items():
        a = np.ascontiguousarray(a)
        arrays[f"in_{name}"] = a
        io[name] = nc.dram_tensor(f"in_{name}", a.shape, mybir.dt.from_np(a.dtype), kind="ExternalInput").ap()
    io["out"] = nc.dram_tensor("out", [NB, SEQ, DM], F32, kind="ExternalOutput").ap()
    program(nc, io)
    r = run_bass_kernel_spmd(nc, [arrays], core_ids=[0])
    return r.results[0]["out"]
```

```python
from contextlib import ExitStack

import concourse.bass as bass
from concourse import mybir
from concourse.alu_op_type import AluOpType as ALU

ACT = mybir.ActivationFunctionType
AX = mybir.AxisListType
F32 = mybir.dt.float32
U32 = mybir.dt.uint32
I32 = mybir.dt.int32

P = 128
DM = 512
KD = DM // P
NB = 4
SEQ = 512
TPB = SEQ // P
NT = NB * TPB
EPS = 1e-5

INNER = 1024
CT = INNER // P
TAPS = 4

NE = 8
FE = 352
FT = [(0, 128), (128, 128), (256, 96)]
NSH = 2
NX = NE + NSH

NH = 16
DH = 128
HG = 4
NG = NH // HG
LEVELS = [2, 4, 8, 16, 32, 64]

FH = 32
NHF = 16


class Program:

    def __init__(self, nc, io):
        self.nc, self.io = nc, io
        self.lasting = ExitStack()
        self.waits_passed = self.lasting.enter_context(nc.semaphore("waits_passed"))
        self.phase_sems = []

    def sem(self, name):
        self.phase_sems.append(self.nc.alloc_semaphore(name=name))
        return self.phase_sems[-1]

    def retire_sems(self):
        with self.nc.Block() as block:
            @block.gpsimd
            def _(e):
                for s in self.phase_sems:
                    e.sem_clear(s)
        for s in self.phase_sems:
            self.nc.release_semaphore(s)
        self.phase_sems = []

    def sb(self, stack, name, shape, dt=F32):
        return stack.enter_context(self.nc.sbuf_tensor(name, shape, dt))

    def ps(self, stack, name, shape, dt=F32):
        return stack.enter_context(self.nc.psum_tensor(name, shape, dt))


class Norm:

    def __init__(self, pr, stack, tag):
        sb = lambda n, s: pr.sb(stack, f"{tag}_{n}", s)
        sem = lambda n: pr.sem(f"{tag}_{n}")
        self.x = sb("x", [P, TPB, DM])
        self.yn = sb("yn", [P, TPB, DM])
        self.st1, self.st2 = sb("st1", [P, TPB, 6]), sb("st2", [P, TPB, 6])
        self.mv1, self.mv2 = sb("mv1", [P, TPB, 2]), sb("mv2", [P, TPB, 2])
        self.ln1, self.ln2 = sb("ln1", [P, TPB]), sb("ln2", [P, TPB])
        self.rs1, self.rs2 = sb("rs1", [P, TPB]), sb("rs2", [P, TPB])
        self.waits_passed = pr.waits_passed
        self.x_loaded = sem("x_loaded")
        self.y_stats = sem("y_stats")
        self.y_mv = sem("y_mv")
        self.y_ln = sem("y_ln")
        self.y_rstd = sem("y_rstd")
        self.y_normed = sem("y_normed")
        self.x_new = sem("x_new")
        self.x_stored = sem("x_stored")
        self.x_stats = sem("x_stats")
        self.x_mv = sem("x_mv")
        self.x_ln = sem("x_ln")
        self.x_rstd = sem("x_rstd")
        self.x_normed = sem("x_normed")
        self.turned = sem("turned")
        self.xt_done = sem("xt_done")


def stand(e, passed):
    e.sem_inc(passed, 1)


def norm_sync(e, n, r, x_old, x_out):
    e.wait_ge(n.x_stored, 16 * r + 1)
    stand(e, n.waits_passed)
    e.wait_ge(n.x_normed, TPB * r + 1)
    stand(e, n.waits_passed)
    e.dma_start(n.x[:, :, :], x_old).then_inc(n.x_loaded, 16)
    e.wait_ge(n.x_new, TPB * r + TPB)
    stand(e, n.waits_passed)
    e.dma_start(x_out, n.x[:, :, :]).then_inc(n.x_stored, 16)


def norm_y_vector(e, n, r, y, wait_y):
    for c in range(TPB):
        wait_y(c)
        e.bn_stats(n.st1[:, c, :], y(c)).then_inc(n.y_stats, 1)
    for c in range(TPB):
        e.wait_ge(n.y_stats, TPB * r + c + 1)
        stand(e, n.waits_passed)
        e.bn_aggr(n.mv1[:, c, :], n.st1[:, c, :]).then_inc(n.y_mv, 1)
    e.wait_ge(n.turned, TPB * r + 1)
    e.wait_ge(n.y_rstd, r + 1)
    for c in range(TPB):
        e.tensor_scalar(n.yn[:, c, :], y(c), n.mv1[:, c, 0:1], n.rs1[:, c:c + 1],
                        ALU.subtract, ALU.mult).then_inc(n.y_normed, 1)
    e.wait_ge(n.x_loaded, 16 * r + 16)
    for c in range(TPB):
        e.wait_ge(n.y_normed, TPB * r + c + 1)
        e.tensor_tensor(n.x[:, c, :], n.x[:, c, :], n.yn[:, c, :], ALU.add).then_inc(n.x_new, 1)


def norm_x_vector(e, n, r, wait_x):
    for c in range(TPB):
        wait_x(c)
        e.bn_stats(n.st2[:, c, :], n.x[:, c, :]).then_inc(n.x_stats, 1)
    for c in range(TPB):
        e.wait_ge(n.x_stats, TPB * r + c + 1)
        stand(e, n.waits_passed)
        e.bn_aggr(n.mv2[:, c, :], n.st2[:, c, :]).then_inc(n.x_mv, 1)
    e.wait_ge(n.turned, TPB * r + 1)
    e.wait_ge(n.x_rstd, r + 1)
    for c in range(TPB):
        e.tensor_scalar(n.yn[:, c, :], n.x[:, c, :], n.mv2[:, c, 0:1], n.rs2[:, c:c + 1],
                        ALU.subtract, ALU.mult).then_inc(n.x_normed, 1)


def norm_y_scalar(e, n, r, eps):
    e.wait_ge(n.y_mv, TPB * r + TPB)
    e.activation(n.ln1[:, :], n.mv1[:, :, 1], ACT.Ln, bias=eps).then_inc(n.y_ln, 1)
    e.wait_ge(n.y_ln, r + 1)
    e.activation(n.rs1[:, :], n.ln1[:, :], ACT.Exp, scale=-0.5).then_inc(n.y_rstd, 1)


def norm_x_scalar(e, n, r, eps, turned, xt):
    e.wait_ge(n.x_mv, TPB * r + TPB)
    e.activation(n.ln2[:, :], n.mv2[:, :, 1], ACT.Ln, bias=eps).then_inc(n.x_ln, 1)
    e.wait_ge(n.x_ln, r + 1)
    e.activation(n.rs2[:, :], n.ln2[:, :], ACT.Exp, scale=-0.5).then_inc(n.x_rstd, 1)
    for c in range(TPB):
        e.wait_ge(n.turned, TPB * r + c + 2)
        e.activation(xt(c), turned[:, :, :], ACT.Copy).then_inc(n.xt_done, 1)


def norm_x_tensor(e, n, r, turned, ident):
    for c in range(TPB):
        e.wait_ge(n.x_normed, TPB * r + c + 2)
        e.wait_ge(n.xt_done, TPB * r + c + 1)
        for k in range(KD):
            mm = e.transpose(turned[:, k, :], n.yn[:, c, k * P:(k + 1) * P], ident)
        mm.then_inc(n.turned, 1)


def norm_start(e, n):
    for s in (n.x_stored, n.x_normed, n.turned, n.xt_done):
        e.sem_inc(s, 1)


def rows(dram, b):
    return dram[b].rearrange("(c p) d -> p c d", p=P)


def constants(pr, stack):
    c = {}
    c["ident"] = pr.sb(stack, "ident", [P, P])
    c["eps"] = pr.sb(stack, "eps", [P, 1])
    for name in ("ones", "before", "upto", "after"):
        c[name] = pr.sb(stack, name, [P, P])
    return c


def phase_first_norm(pr, con, XT):
    nc, io = pr.nc, pr.io
    with ExitStack() as st:
        n = Norm(pr, st, "n0")
        turned = pr.ps(st, "n0_tp", [P, KD, P])
        made = pr.sem("constants_made")
        block = st.enter_context(nc.Block())

        @block.sync
        def _(e):
            with e.Fori(0, NB) as b:
                e.wait_ge(n.x_normed, TPB * b + 1)
                stand(e, pr.waits_passed)
                e.dma_start(n.x[:, :, :], rows(io["x"], b)).then_inc(n.x_loaded, 16)

        @block.gpsimd
        def _(e):
            norm_start(e, n)
            e.memset(con["eps"][:, :], EPS).then_inc(made, 1)
            e.memset(con["ones"][:, :], 1.0).then_inc(made, 1)
            e.memset(con["ident"][:, :], 0.0).then_inc(made, 1)
            e.wait_ge(made, 3)
            e.affine_select(out=con["ident"][:, :], in_=con["ident"][:, :], compare_op=ALU.not_equal,
                            fill=1.0, base=0, pattern=[[-1, P]], channel_multiplier=1).then_inc(made, 1)

        @block.vector
        def _(e):
            with e.Fori(0, NB) as b:
                norm_x_vector(e, n, b, lambda c: e.wait_ge(n.x_loaded, 16 * b + 16))

        @block.scalar
        def _(e):
            e.wait_ge(made, 4)
            with e.Fori(0, NB) as b:
                norm_x_scalar(e, n, b, con["eps"][:, :], turned,
                              lambda c: XT[:, b, :, c * P:(c + 1) * P])

        @block.tensor
        def _(e):
            e.wait_ge(made, 4)
            with e.Fori(0, NB) as b:
                norm_x_tensor(e, n, b, turned, con["ident"][:, :])


def phase_ssm(pr, con, XT):
    nc, io = pr.nc, pr.io
    with ExitStack() as st:
        sb = lambda n, s: pr.sb(st, "a_" + n, s)
        ps = lambda n, s: pr.ps(st, "a_ps_" + n, s)
        sem = lambda n: pr.sem("a_" + n)
        n = Norm(pr, st, "a")
        w_in, w_gate = sb("w_in", [P, KD, INNER]), sb("w_gate", [P, KD, INNER])
        w_out = sb("w_out", [P, CT, DM])
        conv_w, conv_b = sb("conv_w", [P, CT, TAPS]), sb("conv_b", [P, CT])
        dt_b, a_log, dt_w = sb("dt_b", [P, CT]), sb("a_log", [P, CT]), sb("dt_w", [P, CT])
        col_b, col_c, col_d = sb("col_b", [P, CT]), sb("col_c", [P, CT]), sb("col_d", [P, CT])
        exp_a, neg_a = sb("exp_a", [P, CT]), sb("neg_a", [P, CT])
        same_head = sb("same_head", [P, P])
        dt_mat = sb("dt_mat", [P, CT, P])
        conv = sb("conv", [P, 2, SEQ])
        xc, th = sb("xc", [P, CT, SEQ]), sb("th", [P, CT, SEQ])
        soft = sb("soft", [P, 2, SEQ])
        pos = sb("pos", [P, 2, SEQ])
        dt = sb("dt", [P, 2, SEQ])
        decay = sb("decay", [P, 2, SEQ])
        drive = sb("drive", [P, 2, SEQ])
        skip = sb("skip", [P, 2, SEQ])
        state = sb("state", [P, 2, SEQ])
        y = sb("y", [P, TPB, DM])
        pj = [ps(f"pj{i}", [P, SEQ]) for i in range(2)]
        gt = ps("gt", [P, SEQ])
        dtp = [ps(f"dtp{i}", [P, SEQ]) for i in range(2)]
        yo = [ps(f"yo{i}", [P, DM]) for i in range(2)]
        turned = ps("tp", [P, KD, P])
        loaded, cols_loaded = sem("weights_loaded"), sem("columns_loaded")
        head_mask, dt_made, exp_made, neg_made = sem("head_mask"), sem("dt_made"), sem("exp_made"), sem("neg_made")
        pj_ready, gt_ready, dt_ready, yo_ready = sem("pj_ready"), sem("gt_ready"), sem("dt_ready"), sem("yo_ready")
        tap_done = sem("tap_done")
        conv_step = sem("conv_step")
        gt_free = sem("gt_free")
        silu_done = sem("silu_done")
        soft_step = sem("soft_step")
        pos_done = sem("pos_done")
        dt_done = sem("dt_done")
        decay_done = sem("decay_done")
        drive_done = sem("drive_done")
        scan_done = sem("scan_done")
        skip_done = sem("skip_done")
        scaled = sem("scaled")
        gated = sem("gated")
        y_free = sem("y_free")
        block = st.enter_context(nc.Block())

        @block.sync
        def _(e):
            e.dma_start(w_in[:, :, :], io["w_in"]).then_inc(loaded, 16)
            e.dma_start(w_gate[:, :, :], io["w_gate"]).then_inc(loaded, 16)
            for t, name in ((conv_w, "conv_w"), (conv_b, "conv_b"), (dt_b, "dt_b"), (a_log, "a_log"),
                            (dt_w, "dt_w"), (col_b, "col_b"), (col_c, "col_c"), (col_d, "col_d")):
                e.dma_start(t[:], io[name]).then_inc(cols_loaded, 16)
            e.dma_start(w_out[:, :, :], io["w_out"]).then_inc(loaded, 16)
            with e.Fori(0, NB) as b:
                norm_sync(e, n, b, rows(io["x"], b), rows(io["x1"], b))
            e.wait_ge(n.x_stored, 16 * NB + 1)

        @block.gpsimd
        def _(e):
            norm_start(e, n)
            for s, k in ((conv_step, 2 * (TAPS - 1)), (gt_free, 1), (silu_done, 2), (pos_done, 2), (scaled, 2), (y_free, 2)):
                e.sem_inc(s, k)
            e.memset(same_head[:, :], 0.0).then_inc(head_mask, 1)
            e.wait_ge(head_mask, 1)
            e.memset(same_head[0:64, 0:64], 1.0).then_inc(head_mask, 1)
            e.memset(same_head[64:128, 64:128], 1.0).then_inc(head_mask, 1)
            e.wait_ge(head_mask, 3)
            e.wait_ge(cols_loaded, 16 * 8)
            for c in range(CT):
                e.tensor_scalar(dt_mat[:, c, :], same_head[:, :], dt_w[:, c:c + 1], None, ALU.mult).then_inc(dt_made, 1)
            with e.Fori(0, NB) as b:
                for c in range(CT):
                    e.wait_ge(silu_done, b * CT + c + 3)
                    e.wait_ge(scaled, b * CT + c + 1)
                    stand(e, pr.waits_passed)
                    e.tensor_scalar(skip[:, c % 2, :], xc[:, c, :], col_d[:, c:c + 1], None, ALU.mult).then_inc(skip_done, 1)

        @block.tensor
        def _(e):
            e.wait_ge(loaded, 48)
            e.wait_ge(dt_made, CT)
            with e.Fori(0, NB) as b:
                def project(c):
                    e.wait_ge(conv_step, (b * CT + c + 1) * (TAPS - 1))
                    for k in range(KD):
                        mm = e.matmul(pj[c % 2][:, :], w_in[:, k, c * P:(c + 1) * P], XT[:, b, k, :],
                                      start=(k == 0), stop=(k == KD - 1))
                    mm.then_inc(pj_ready, 1)
                    e.wait_ge(gt_free, b * CT + c + 1)
                    for k in range(KD):
                        mm = e.matmul(gt[:, :], w_gate[:, k, c * P:(c + 1) * P], XT[:, b, k, :],
                                      start=(k == 0), stop=(k == KD - 1))
                    mm.then_inc(gt_ready, 1)

                def step_sizes(c):
                    e.wait_ge(silu_done, b * CT + c + 3)
                    e.wait_ge(pos_done, b * CT + c + 1)
                    e.matmul(dtp[c % 2][:, :], dt_mat[:, c, :], xc[:, c, :], start=True, stop=True).then_inc(dt_ready, 1)

                for c in range(5):
                    project(c)
                for c in range(4):
                    step_sizes(c)
                for c in range(5, CT):
                    project(c)
                for c in range(4, CT):
                    step_sizes(c)
                for t in range(TPB):
                    e.wait_ge(y_free, b * TPB + t + 1)
                    for c in range(CT):
                        if t == 0:
                            e.wait_ge(gated, b * CT + c + 1)
                        mm = e.matmul(yo[t % 2][:, :], th[:, c, t * P:(t + 1) * P], w_out[:, c, :],
                                      start=(c == 0), stop=(c == CT - 1))
                    mm.then_inc(yo_ready, 1)
                norm_x_tensor(e, n, b, turned, con["ident"][:, :])

        @block.scalar
        def _(e):
            e.wait_ge(cols_loaded, 16 * 8)
            e.activation(exp_a[:, :], a_log[:, :], ACT.Exp).then_inc(exp_made, 1)
            e.wait_ge(neg_made, 1)
            with e.Fori(0, NB) as b:
                def silu(c):
                    e.wait_ge(conv_step, (b * CT + c + 3) * (TAPS - 1))
                    e.activation(xc[:, c, :], conv[:, c % 2, :], ACT.Silu).then_inc(silu_done, 1)

                def first(c):
                    e.wait_ge(pj_ready, b * CT + c + 1)
                    e.wait_ge(silu_done, b * CT + c + 1)
                    e.activation(conv[:, c % 2, :], pj[c % 2][:, :], ACT.Identity, bias=conv_b[:, c:c + 1],
                                 scale=conv_w[:, c, TAPS - 1:TAPS]).then_inc(tap_done, 1)
                    e.wait_ge(gt_ready, b * CT + c + 1)
                    e.activation(th[:, c, :], gt[:, :], ACT.Tanh, scale=0.5).then_inc(gt_free, 1)

                def step_size(c):
                    z, s = dtp[c % 2][:, :], soft[:, c % 2, :]
                    m = 3 * (b * CT + c)
                    e.wait_ge(dt_ready, b * CT + c + 1)
                    if c >= 2:
                        e.wait_ge(dt_done, b * CT + c - 1)
                    e.activation(s, z, ACT.Abs, bias=dt_b[:, c:c + 1]).then_inc(soft_step, 1)
                    e.activation(pos[:, c % 2, :], z, ACT.Relu, bias=dt_b[:, c:c + 1]).then_inc(pos_done, 1)
                    e.wait_ge(soft_step, m + 1)
                    e.activation(s, s, ACT.Exp, scale=-1.0).then_inc(soft_step, 1)
                    e.wait_ge(soft_step, m + 2)
                    e.activation(s, s, ACT.Ln, bias=1.0).then_inc(soft_step, 1)

                def decays(c):
                    e.wait_ge(dt_done, b * CT + c + 1)
                    if c >= 2:
                        e.wait_ge(scan_done, b * CT + c - 1)
                    e.activation(decay[:, c % 2, :], dt[:, c % 2, :], ACT.Exp, scale=neg_a[:, c:c + 1]).then_inc(decay_done, 1)

                def half(lo, hi):
                    e.preload_act_table_set("natural_log_exp_and_others")
                    for c in range(lo, hi):
                        step_size(c)
                        if c > lo:
                            decays(c - 1)
                    decays(hi - 1)

                first(0)
                for c in range(1, 4):
                    first(c)
                    silu(c - 1)
                silu(3)
                first(4)
                half(0, 4)
                for c in range(5, CT):
                    first(c)
                    silu(c - 1)
                silu(CT - 1)
                half(4, CT)
                for t in range(TPB):
                    e.wait_ge(yo_ready, b * TPB + t + 1)
                    e.activation(y[:, t, :], yo[t % 2][:, :], ACT.Copy, scale=0.5).then_inc(y_free, 1)
                norm_y_scalar(e, n, b, con["eps"][:, :])
                norm_x_scalar(e, n, b, con["eps"][:, :], turned, lambda c: XT[:, b, :, c * P:(c + 1) * P])

        @block.vector
        def _(e):
            e.wait_ge(exp_made, 1)
            e.tensor_scalar(neg_a[:, :], exp_a[:, :], -1.0, None, ALU.mult).then_inc(neg_made, 1)
            with e.Fori(0, NB) as b:
                def taps(c):
                    e.wait_ge(tap_done, b * CT + c + 1)
                    for s in range(1, TAPS):
                        m = (b * CT + c + 2) * (TAPS - 1) + s - 1
                        if s > 1:
                            e.wait_ge(conv_step, m)
                        o = conv[:, c % 2, s:SEQ]
                        e.scalar_tensor_tensor(o, pj[c % 2][:, 0:SEQ - s], conv_w[:, c, TAPS - 1 - s:TAPS - s], o,
                                                     ALU.mult, ALU.add).then_inc(conv_step, 1)

                def scan(c):
                    m, i = b * CT + c, c % 2
                    e.wait_ge(soft_step, 3 * m + 3)
                    e.wait_ge(pos_done, m + 3)
                    e.tensor_tensor(dt[:, i, :], soft[:, i, :], pos[:, i, :], ALU.add).then_inc(dt_done, 1)
                    e.wait_ge(dt_done, m + 1)
                    e.wait_ge(silu_done, m + 3)
                    e.scalar_tensor_tensor(drive[:, i, :], dt[:, i, :], col_b[:, c:c + 1], xc[:, c, :],
                                           ALU.mult, ALU.mult).then_inc(drive_done, 1)
                    e.wait_ge(decay_done, m + 1)
                    e.wait_ge(drive_done, m + 1)
                    e.tensor_tensor_scan(state[:, i, :], decay[:, i, :], drive[:, i, :], 0.0,
                                         ALU.mult, ALU.add).then_inc(scan_done, 1)
                    e.wait_ge(scan_done, m + 1)
                    e.wait_ge(skip_done, m + 1)
                    e.scalar_tensor_tensor(state[:, i, :], state[:, i, :], col_c[:, c:c + 1], skip[:, i, :],
                                           ALU.mult, ALU.add).then_inc(scaled, 1)
                    e.wait_ge(scaled, m + 3)
                    e.wait_ge(gt_free, m + 2)
                    e.scalar_tensor_tensor(th[:, c, :], th[:, c, :], 1.0, state[:, i, :],
                                           ALU.add, ALU.mult).then_inc(gated, 1)

                for c in range(5):
                    taps(c)
                for c in range(4):
                    scan(c)
                for c in range(5, CT):
                    taps(c)
                for c in range(4, CT):
                    scan(c)
                norm_y_vector(e, n, b, lambda c: y[:, c, :], lambda c: e.wait_ge(y_free, b * TPB + c + 3))
                norm_x_vector(e, n, b, lambda c: e.wait_ge(n.x_new, TPB * b + c + 1))


def top2(e, score, shape, t, route, start):
    wide = lambda a: a.unsqueeze(2).to_broadcast(shape)
    prefer = t["prefer"][:, :].unsqueeze(1).to_broadcast(shape)
    n = start

    def after():
        e.wait_ge(route, n)

    rest = score
    for one in ("one1", "one2"):
        after()
        e.tensor_reduce(t["top"][:, :], rest, AX.X, ALU.max).then_inc(route, 1)
        n += 1
        after()
        e.tensor_tensor(t["key"][:, :, :], rest, wide(t["top"][:, :]), ALU.is_equal).then_inc(route, 1)
        n += 1
        after()
        e.tensor_tensor(t["key"][:, :, :], t["key"][:, :, :], prefer, ALU.mult).then_inc(route, 1)
        n += 1
        after()
        e.tensor_reduce(t["top"][:, :], t["key"][:, :, :], AX.X, ALU.max).then_inc(route, 1)
        n += 1
        after()
        e.tensor_tensor(t[one][:, :, :], t["key"][:, :, :], wide(t["top"][:, :]), ALU.is_equal).then_inc(route, 1)
        n += 1
        if one == "one1":
            after()
            e.scalar_tensor_tensor(t["rest"][:, :, :], t["one1"][:, :, :], -2.0, score, ALU.mult, ALU.add).then_inc(route, 1)
            n += 1
            rest = t["rest"][:, :, :]
    return n


def softmax_front(e, logits, t, shape, route, start):
    e.wait_ge(route, start)
    e.tensor_reduce(t["top"][:, :], logits, AX.X, ALU.max).then_inc(route, 1)
    e.wait_ge(route, start + 1)
    e.tensor_tensor(t["score"][:, :, :], logits, t["top"][:, :].unsqueeze(2).to_broadcast(shape), ALU.subtract).then_inc(route, 1)
    return start + 2


def softmax_back(e, t, shape, route, start):
    e.wait_ge(route, start)
    e.tensor_reduce(t["top"][:, :], t["score"][:, :, :], AX.X, ALU.add).then_inc(route, 1)
    e.wait_ge(route, start + 1)
    e.reciprocal(t["inv"][:, :], t["top"][:, :]).then_inc(route, 1)
    e.wait_ge(route, start + 2)
    e.tensor_tensor(t["score"][:, :, :], t["score"][:, :, :], t["inv"][:, :].unsqueeze(2).to_broadcast(shape), ALU.mult).then_inc(route, 1)
    return start + 3


def route_tiles(sb, rows_n):
    t = {k: sb(k, [P, rows_n, NE]) for k in ("score", "key", "rest", "one1", "one2")}
    t["top"], t["inv"] = sb("top", [P, rows_n]), sb("inv", [P, rows_n])
    t["prefer"] = sb("prefer", [P, NE])
    return t


def phase_moe(pr, con, XT):
    nc, io = pr.nc, pr.io
    with ExitStack() as st:
        sb = lambda n, s: pr.sb(st, "b_" + n, s)
        ps = lambda n, s: pr.ps(st, "b_ps_" + n, s)
        sem = lambda n: pr.sem("b_" + n)
        n = Norm(pr, st, "b")
        shape = [P, NT, NE]
        t = route_tiles(sb, NT)
        gate_w = sb("gate_w", [P, KD, NE])
        comb = sb("comb", [P, NT, NX])
        acc = sb("acc", [P, NT, DM])
        w_gu = [sb(f"w_gu{i}", [P, KD, 2 * FE]) for i in range(2)]
        w_dn = [sb(f"w_dn{i}", [P, len(FT), DM]) for i in range(2)]
        hs = [sb(f"hs{i}", [P, SEQ]) for i in range(2)]
        act = sb("act", [P, len(FT), SEQ])
        g_ps = [ps(f"g{i}", [P, SEQ]) for i in range(2)]
        u_ps = [ps(f"u{i}", [P, SEQ]) for i in range(2)]
        y_ps = [ps(f"y{i}", [P, DM]) for i in range(TPB)]
        logits = y_ps[0][:, 0:NT * NE].rearrange("p (t e) -> p t e", e=NE)
        turned = g_ps[0][:, :].rearrange("p (k t) -> p k t", k=KD)
        gate_loaded = sem("gate_loaded")
        w_loaded = [sem("w_loaded0"), sem("w_loaded1")]
        prefer_made, zeroed = sem("prefer_made"), sem("zeroed")
        logits_ready = sem("logits_ready")
        route = sem("route")
        comb_done = sem("comb_done")
        g_ready, u_ready = sem("g_ready"), sem("u_ready")
        silu_done = sem("silu_done")
        act_done = sem("act_done")
        y_ready = sem("y_ready")
        acc_done = sem("acc_done")
        xt_stored = sem("xt_stored")
        block = st.enter_context(nc.Block())

        def load_expert(e, x, par):
            e.dma_start(w_gu[par][:, :, :], io["w_gu"][x]).then_inc(w_loaded[par], 16)
            e.dma_start(w_dn[par][:, 0:2, :], io["w_dn"][x][:, 0:2, :]).then_inc(w_loaded[par], 16)
            e.dma_start(w_dn[par][0:FT[2][1], 2, :], io["w_dn"][x][0:FT[2][1], 2, :]).then_inc(w_loaded[par], 16)

        @block.sync
        def _(e):
            e.dma_start(gate_w[:, :, :], io["gate_w"]).then_inc(gate_loaded, 16)
            for par in range(2):
                load_expert(e, par, par)
            with e.Fori(1, NX // 2) as xp:
                for par in range(2):
                    e.wait_ge(y_ready, (xp * 2 + par - 1) * NT)
                    stand(e, pr.waits_passed)
                    load_expert(e, xp * 2 + par, par)
            with e.Fori(0, NB) as b:
                norm_sync(e, n, b, rows(io["x1"], b), rows(io["x2"], b))
                e.wait_ge(n.xt_done, TPB * b + TPB + 1)
                stand(e, pr.waits_passed)
                e.dma_start(io["xt_d"][b], XT[:, b, :, :]).then_inc(xt_stored, 16)
                e.wait_ge(xt_stored, 16 * b + 16)
                stand(e, pr.waits_passed)
            e.wait_ge(n.x_stored, 16 * NB + 1)

        @block.gpsimd
        def _(e):
            norm_start(e, n)
            for s, k in ((route, 1), (act_done, 3), (acc_done, 4)):
                e.sem_inc(s, k)
            for x in range(NE):
                e.memset(t["prefer"][:, x:x + 1], float(NE - x)).then_inc(prefer_made, 1)
            e.memset(comb[:, :, NE:NX], 1.0).then_inc(zeroed, 1)
            e.memset(acc[:, :, :], 0.0).then_inc(zeroed, 1)

        @block.tensor
        def _(e):
            e.wait_ge(gate_loaded, 16)
            for b in range(NB):
                for c in range(TPB):
                    for k in range(KD):
                        mm = e.matmul(logits[:, b * TPB + c, :], XT[:, b, k, c * P:(c + 1) * P], gate_w[:, k, :],
                                      start=(k == 0), stop=(k == KD - 1))
            mm.then_inc(logits_ready, 1)
            e.wait_ge(route, 3)
            with e.Fori(0, NX // 2) as xp:
                for par in range(2):
                    e.wait_ge(w_loaded[par], 48 * xp + 48)
                    stand(e, pr.waits_passed)
                    with e.Fori(0, NB) as b:
                        u = (xp * 2 + par) * NB + b
                        for f, (lo, width) in enumerate(FT):
                            e.wait_ge(act_done, 3 * u + (3, 3, 4)[f])
                            for dst, at, ready in ((g_ps, lo, g_ready), (u_ps, FE + lo, u_ready)):
                                for k in range(KD):
                                    mm = e.matmul(dst[f % 2][0:width, :], w_gu[par][:, k, at:at + width], XT[:, b, k, :],
                                                  start=(k == 0), stop=(k == KD - 1))
                                mm.then_inc(ready, 1)

                        def down(c, f):
                            return e.matmul(y_ps[c][:, :], act[0:FT[f][1], f, c * P:(c + 1) * P],
                                            w_dn[par][0:FT[f][1], f, :], start=(f == 0), stop=(f == len(FT) - 1))

                        e.wait_ge(act_done, 3 * u + 5)
                        for c in range(TPB):
                            e.wait_ge(acc_done, TPB * u + c + 1)
                            for f in range(2):
                                down(c, f)
                        e.wait_ge(act_done, 3 * u + 6)
                        for c in range(TPB):
                            down(c, 2).then_inc(y_ready, 1)
            with e.Fori(0, NB) as b:
                norm_x_tensor(e, n, b, turned, con["ident"][:, :])

        @block.scalar
        def _(e):
            e.wait_ge(route, 3)
            e.activation(t["score"][:, :, :], t["score"][:, :, :], ACT.Exp).then_inc(route, 1)
            with e.Fori(0, NX // 2) as xp:
                for par in range(2):
                    with e.Fori(0, NB) as b:
                        u = (xp * 2 + par) * NB + b
                        for f, (lo, width) in enumerate(FT):
                            e.wait_ge(g_ready, 3 * u + f + 1)
                            e.activation(hs[f % 2][0:width, :], g_ps[f % 2][0:width, :], ACT.Silu).then_inc(silu_done, 1)
            with e.Fori(0, NB) as b:
                norm_y_scalar(e, n, b, con["eps"][:, :])
                norm_x_scalar(e, n, b, con["eps"][:, :], turned, lambda c: XT[:, b, :, c * P:(c + 1) * P])

        @block.vector
        def _(e):
            e.wait_ge(prefer_made, NE)
            e.wait_ge(logits_ready, 1)
            m = softmax_front(e, logits, t, shape, route, 1)
            m = softmax_back(e, t, shape, route, m + 1)
            m = top2(e, t["score"][:, :, :], shape, t, route, m)
            e.wait_ge(route, m)
            e.tensor_tensor(t["one1"][:, :, :], t["one1"][:, :, :], t["one2"][:, :, :], ALU.add).then_inc(route, 1)
            e.wait_ge(route, m + 1)
            e.wait_ge(zeroed, 2)
            e.tensor_tensor(comb[:, :, 0:NE], t["one1"][:, :, :], t["score"][:, :, :], ALU.mult).then_inc(comb_done, 1)
            e.wait_ge(comb_done, 1)
            with e.Fori(0, NX // 2) as xp:
                for par in range(2):
                    with e.Fori(0, NB) as b:
                        u = (xp * 2 + par) * NB + b
                        for f, (lo, width) in enumerate(FT):
                            e.wait_ge(u_ready, 3 * u + f + 1)
                            e.wait_ge(silu_done, 3 * u + f + 1)
                            e.tensor_tensor(act[0:width, f, :], hs[f % 2][0:width, :], u_ps[f % 2][0:width, :], ALU.mult).then_inc(act_done, 1)
                        for c in range(TPB):
                            e.wait_ge(y_ready, TPB * u + c + 1)
                            tile = acc[:, b * TPB + c, :]
                            weight = comb[:, :, :].unsqueeze(3)[:, b * TPB + c, xp * 2 + par, :]
                            e.scalar_tensor_tensor(tile, y_ps[c][:, :], weight, tile, ALU.mult, ALU.add).then_inc(acc_done, 1)
            with e.Fori(0, NB) as b:
                norm_y_vector(e, n, b, lambda c: acc[:, b * TPB + c, :],
                              lambda c: e.wait_ge(acc_done, NX * NT + 4))
                norm_x_vector(e, n, b, lambda c: e.wait_ge(n.x_new, TPB * b + c + 1))


def gate_tables(pr, stack):
    return {k: pr.sb(stack, k + "_all", [P, NG, NB, TPB, HG]) for k in
            ("beta", "log_decay", "decay_before", "decay_upto", "decay_all")}


def phase_gates(pr, con, XT, tab):
    nc, io = pr.nc, pr.io
    with ExitStack() as st:
        sb = lambda n, s: pr.sb(st, "g_" + n, s)
        sem = lambda n: pr.sem("g_" + n)
        w_ab, bias = sb("w_ab", [P, KD, 2 * NH]), sb("bias", [P, 2 * NH])
        z = sb("z", [P, NT, 2 * NH])
        soft = sb("soft", [P, NT, NH])
        z_ps = pr.ps(st, "g_z_ps", [P, NT, 2 * NH])
        cum_ps = [pr.ps(st, f"g_cum{i}", [P, NT * NH]) for i in range(3)]
        by_group = lambda t, b: t[:, :, b].rearrange("p g c h -> p c g h")
        heads_of = lambda a, b, first: a[:, b * TPB:(b + 1) * TPB, first:first + NH].rearrange("p c (g h) -> p c g h", h=HG)
        loaded, masks, z_ready, z_done = sem("loaded"), sem("masks"), sem("z_ready"), sem("z_done")
        soft_step, la_done, cum_ready = sem("soft_step"), sem("la_done"), sem("cum_ready")
        block = st.enter_context(nc.Block())

        @block.sync
        def _(e):
            e.dma_start(w_ab[:, :, :], io["w_ab"]).then_inc(loaded, 16)
            e.dma_start(bias[:, :], io["b_ab"].partition_broadcast(P)).then_inc(loaded, 16)

        @block.gpsimd
        def _(e):
            for name, base, mul, step in (("before", 0, -1, 1), ("upto", 1, -1, 1), ("after", 0, 1, -1)):
                e.affine_select(out=con[name][:, :], in_=con["ones"][:, :], compare_op=ALU.is_gt, fill=0.0,
                                base=base, pattern=[[step, P]], channel_multiplier=mul).then_inc(masks, 1)

        @block.tensor
        def _(e):
            e.wait_ge(loaded, 32)
            for b in range(NB):
                for c in range(TPB):
                    for k in range(KD):
                        mm = e.matmul(z_ps[:, b * TPB + c, :], XT[:, b, k, c * P:(c + 1) * P], w_ab[:, k, :],
                                      start=(k == 0), stop=(k == KD - 1))
            mm.then_inc(z_ready, 1)
            e.wait_ge(masks, 3)
            e.wait_ge(la_done, NB * NG)
            for dst, mask in zip(cum_ps, ("before", "upto", "ones")):
                e.matmul(dst[:, :], con[mask][:, :], tab["log_decay"][:, :, :, :, :].rearrange("p g b c h -> p (g b c h)"),
                         start=True, stop=True).then_inc(cum_ready, 1)

        @block.scalar
        def _(e):
            e.wait_ge(z_done, 1)
            for b in range(NB):
                e.activation(by_group(tab["beta"], b), heads_of(z, b, NH), ACT.Sigmoid)
            e.preload_act_table_set("natural_log_exp_and_others")
            e.activation(soft[:, :, :], z[:, :, 0:NH], ACT.Abs).then_inc(soft_step, 1)
            e.wait_ge(soft_step, 1)
            e.activation(soft[:, :, :], soft[:, :, :], ACT.Exp, scale=-1.0).then_inc(soft_step, 1)
            e.wait_ge(soft_step, 2)
            e.activation(soft[:, :, :], soft[:, :, :], ACT.Ln, bias=1.0).then_inc(soft_step, 1)
            for i, name in enumerate(("decay_before", "decay_upto", "decay_all")):
                e.wait_ge(cum_ready, i + 1)
                e.activation(tab[name][:, :, :, :, :].rearrange("p g b c h -> p (g b c h)"), cum_ps[i][:, :], ACT.Exp)

        @block.vector
        def _(e):
            e.wait_ge(z_ready, 1)
            e.wait_ge(loaded, 32)
            e.tensor_tensor(z[:, :, :], z_ps[:, :, :], bias[:, :].unsqueeze(1).to_broadcast([P, NT, 2 * NH]), ALU.add).then_inc(z_done, 1)
            e.wait_ge(z_done, 1)
            e.wait_ge(soft_step, 3)
            for b in range(NB):
                for g in range(NG):
                    e.scalar_tensor_tensor(by_group(tab["log_decay"], b)[:, :, g], heads_of(z, b, 0)[:, :, g], 0.0,
                                           heads_of(soft, b, 0)[:, :, g], ALU.min, ALU.subtract).then_inc(la_done, 1)


def halves(ap, m):
    v = ap.rearrange("p h (n two m) -> p h n two m", two=2, m=m)
    return v[:, :, :, 0, :], v[:, :, :, 1, :]


def phase_delta(pr, con, tab):
    nc, io = pr.nc, pr.io
    HC = HG * DH
    H4 = [P, HG, P]
    NR = NG * NB
    NP = TPB + 3 * HG
    TAP_STEPS = TAPS - 1
    CONVS = 3 * HG
    NL = len(LEVELS)
    with ExitStack() as st:
        sb = lambda n, s: pr.sb(st, "c_" + n, s)
        ps = lambda n, s: pr.ps(st, "c_ps_" + n, s)
        sem = lambda n: pr.sem("c_" + n)
        w = {m: sb("w_" + m, [P, KD, HC]) for m in "gkqv"}
        conv_w = {m: sb("conv_w" + m, [P, HG, TAPS]) for m in "kqv"}
        conv_b = {m: sb("conv_b" + m, [P, HG]) for m in "kqv"}
        ln_w, ln_b = sb("ln_w", [P, DH]), sb("ln_b", [P, DH])
        xs = sb("xs", [P, KD, SEQ])
        heads = [{m: sb(f"{m}T{i}", [P, HG, SEQ]) for m in "kqv"} for i in range(2)]
        gates = [sb(f"gate{i}", [P, TPB, HG, DH]) for i in range(2)]
        conv = sb("conv", [P, 2, SEQ])
        beta, log_decay, before, upto, whole = (sb(k, [P, TPB, HG]) for k in ("beta", "log_decay", "before", "upto", "whole"))
        masked_la, masked_b = sb("masked_la", [P, 2, HG, P]), sb("masked_b", [P, 2, HG, P])
        decay = sb("decay", [P, HG, P])
        G = sb("G", [P, 2, HG, P])
        negL = sb("negL", [P, TPB, HG, P])
        A = sb("A", [P, TPB, HG, P])
        R, T = sb("R", [P, TPB, HG, P]), sb("T", [P, TPB, HG, P])
        Z = sb("Z", [P, TPB, HG, P])
        kd = sb("kd", [P, TPB, HG, DH])
        negv = sb("negv", [P, TPB, HG, DH])
        S = sb("S", [P, HG, DH])
        err = sb("err", [P, HG, DH])
        o = sb("o", [P, 2, HG, DH])
        on = sb("on", [P, HG, DH])
        oT = sb("oT", [P, HG, P])
        o_st, o_mv = sb("o_st", [P, HG, 6]), sb("o_mv", [P, HG, 2])
        o_ve, o_t, o_rs = sb("o_ve", [P, HG]), sb("o_t", [P, HG]), sb("o_rs", [P, HG])
        mask_R = [sb(f"mask_R{m}", [P, P // 2]) for m in LEVELS]
        mask_T = [sb(f"mask_T{m}", [P, P // 2]) for m in LEVELS[:-1]]
        pair = sb("pair", [P, P])
        pj = [ps(f"pj{i}", [P, SEQ]) for i in range(2)]
        kk_ps, kq_ps, d_ps, z_ps, r_ps, t_ps = (ps(k, [P, SEQ]) for k in ("kk", "kq", "d", "z", "r", "t"))
        by_head = lambda bank: bank[:, :].rearrange("p (h m) -> p h m", h=HG)
        kk, kq, d4, z4, r4, t4 = (by_head(x) for x in (kk_ps, kq_ps, d_ps, z_ps, r_ps, t_ps))
        p4 = [by_head(x) for x in pj]
        half_of = lambda bank: bank[:, 0:HG * P // 2].rearrange("p (h m) -> p h m", h=HG)
        z_half = [half_of(z_ps), half_of(d_ps)]
        r_half = [half_of(r_ps), half_of(kk_ps)]
        t_half = [half_of(t_ps), half_of(kq_ps)]
        on_heads = lambda a, c: a[:, c, :].unsqueeze(2).to_broadcast(H4)
        over_heads = lambda m: m[:, :].unsqueeze(1).to_broadcast(H4)

        w_loaded, ln_loaded, xs_loaded = sem("w_loaded"), sem("ln_loaded"), sem("xs_loaded")
        masks_made, cleared = sem("masks_made"), sem("cleared")
        tables = sem("tables")
        pj_ready = sem("pj_ready")
        tap_done = sem("tap_done")
        conv_step = sem("conv_step")
        silu_done = sem("silu_done")
        k_scaled = sem("k_scaled")
        g_copied, g_done = sem("g_copied"), sem("g_done")
        la_masked, b_masked = sem("la_masked"), sem("b_masked")
        d_ready, decay_done, G_done = sem("d_ready"), sem("decay_done"), sem("G_done")
        kk_ready, L_done, A_done = sem("kk_ready"), sem("L_done"), sem("A_done")
        R_step = sem("R_step")
        rt_ready, T_done = sem("rt_ready"), sem("T_done")
        kt_ready, kd_done, vt_ready, v_done = sem("kt_ready"), sem("kd_done"), sem("vt_ready"), sem("v_done")
        zl_ready, zl_done = sem("zl_ready"), sem("zl_done")
        rl_ready, rl_done = sem("rl_ready"), sem("rl_done")
        tl_ready, tl_done = sem("tl_ready"), sem("tl_done")
        kS_ready, v_less = sem("kS_ready"), sem("v_less")
        qS_ready, qS_done = sem("qS_ready"), sem("qS_done")
        err_ready, err_done = sem("err_ready"), sem("err_done")
        dS_ready, S_done = sem("dS_ready"), sem("S_done")
        Ae_ready, o_done = sem("Ae_ready"), sem("o_done")
        o_stats, o_mean, o_rstd = sem("o_stats"), sem("o_mean"), sem("o_rstd")
        o_normed = sem("o_normed")
        o_gated = sem("o_gated")
        ot_ready = sem("ot_ready")
        ot_done = sem("ot_done")
        ot_stored = sem("ot_stored")
        RSTD_STEPS = 15
        block = st.enter_context(nc.Block())

        def rounds(e, first, each, last):
            first()
            each(0, 0)
            with e.Fori(0, NR // 2 - 1) as p:
                each(p * 2 + 1, 1)
                each(p * 2 + 2, 0)
            last(NR - 1, 1)

        @block.sync
        def _(e):
            e.dma_start(ln_w[:, :], io["ln_w"].partition_broadcast(P)).then_inc(ln_loaded, 16)
            e.dma_start(ln_b[:, :], io["ln_b"].partition_broadcast(P)).then_inc(ln_loaded, 16)

            def load_weights(hg, wait_used):
                for i, m in enumerate("gkqv"):
                    wait_used(i)
                    e.dma_start(w[m][:, :, :], io["w_" + m][hg]).then_inc(w_loaded, 16)
                for m in "kqv":
                    e.dma_start(conv_w[m][:, :, :], io["conv_w" + m][hg]).then_inc(w_loaded, 16)
                    e.dma_start(conv_b[m][:, :], io["conv_b" + m][hg]).then_inc(w_loaded, 16)
                e.wait_ge(w_loaded, 160 * hg + 160)
                stand(e, pr.waits_passed)

            def load_x(q, b):
                e.wait_ge(pj_ready, NP * q)
                stand(e, pr.waits_passed)
                e.dma_start(xs[:, :, :], io["xt_d"][b]).then_inc(xs_loaded, 16)

            load_weights(0, lambda i: None)
            e.dma_start(xs[:, :, :], io["xt_d"][0]).then_inc(xs_loaded, 16)
            with e.Fori(1, NB) as b:
                load_x(b, b)
            with e.Fori(1, NG) as hg:
                def wait_used(i):
                    e.wait_ge(pj_ready, NP * NB * hg - NP + HG * (i + 1))
                    stand(e, pr.waits_passed)
                    if i == 3:
                        e.wait_ge(conv_step, CONVS * TAP_STEPS * NB * hg + 2 * TAP_STEPS)
                        stand(e, pr.waits_passed)
                load_weights(hg, wait_used)
                with e.Fori(0, NB) as b:
                    load_x(hg * NB + b, b)

        @block.gpsimd
        def _(e):
            for s, k in ((conv_step, 2 * TAP_STEPS), (silu_done, 2), (ot_done, 2), (ot_stored, 16)):
                e.sem_inc(s, k)
            made = 0
            for l, m in enumerate(LEVELS):
                for mask, odd in ((mask_R, 0),) + (((mask_T, 1),) if m < P // 2 else ()):
                    a = mask[l][:, :].rearrange("p (n m) -> p n m", m=m)
                    o1 = con["ones"][:, 0:P // 2].rearrange("p (n m) -> p n m", m=m)
                    lo = odd * m
                    e.affine_select(out=a, in_=o1, compare_op=ALU.is_ge, fill=0.0, base=-lo,
                                    pattern=[[-2 * m, P // 2 // m], [0, m]], channel_multiplier=1).then_inc(masks_made, 1)
                    made += 1
                    e.wait_ge(masks_made, made)
                    e.affine_select(out=a, in_=a, compare_op=ALU.is_gt, fill=0.0, base=lo + m,
                                    pattern=[[2 * m, P // 2 // m], [0, m]], channel_multiplier=-1).then_inc(masks_made, 1)
                    made += 1
            pv = pair[:, :].rearrange("p (n two) -> p n two", two=2)
            ov = con["ones"][:, :].rearrange("p (n two) -> p n two", two=2)
            e.memset(pair[:, :], 0.0).then_inc(masks_made, 1)
            made += 1
            e.wait_ge(masks_made, made)
            e.affine_select(out=pv[:, :, 1], in_=ov[:, :, 1], compare_op=ALU.is_equal, fill=0.0, base=0,
                            pattern=[[-2, P // 2]], channel_multiplier=1).then_inc(masks_made, 1)
            made += 1
            e.wait_ge(masks_made, made)
            for a in (negL, Z):
                e.memset(a[:, :, :, :], 0.0).then_inc(cleared, 1)
            e.wait_ge(cleared, 2)
            e.wait_ge(ln_loaded, 32)

            def copy_tables(r):
                for dst, name in ((beta, "beta"), (log_decay, "log_decay"), (before, "decay_before"),
                                  (upto, "decay_upto"), (whole, "decay_all")):
                    src = tab[name][:, :, :, :, :].rearrange("p g b c h -> p (g b) c h")
                    e.tensor_copy(dst[:, :, :].unsqueeze(1), src[:, bass.ds(r, 1)]).then_inc(tables, 1)
                e.wait_ge(tables, 5 * r + 5)
                stand(e, pr.waits_passed)

            def mask_gates(r, c):
                if c >= 2:
                    e.wait_ge(d_ready, r * TPB + c - 1)
                    stand(e, pr.waits_passed)
                e.tensor_tensor(masked_la[:, c % 2], on_heads(log_decay, c), over_heads(con["upto"]), ALU.mult).then_inc(la_masked, 1)
                if c >= 2:
                    e.wait_ge(G_done, r * TPB + c - 1)
                    stand(e, pr.waits_passed)
                e.tensor_tensor(masked_b[:, c % 2], on_heads(beta, c), over_heads(con["upto"]), ALU.mult).then_inc(b_masked, 1)

            def finish_projections(q, buf):
                for c in range(TPB):
                    e.wait_ge(g_copied, q * TPB + c + 1)
                    stand(e, pr.waits_passed)
                    e.tensor_scalar(gates[buf][:, c], gates[buf][:, c], 0.5, 0.5, ALU.mult, ALU.add).then_inc(g_done, 1)
                for h in range(HG):
                    e.wait_ge(silu_done, CONVS * q + h + 3)
                    stand(e, pr.waits_passed)
                    e.tensor_scalar(heads[buf]["k"][:, h, :], heads[buf]["k"][:, h, :], DH ** -0.5, None, ALU.mult).then_inc(k_scaled, 1)

            def gate_out(r, buf, c):
                n = r * TPB + c
                e.wait_ge(o_normed, HG * n + HG)
                e.wait_ge(g_done, n + 1)
                stand(e, pr.waits_passed)
                for i, (b, op) in enumerate(((over_heads(ln_w), ALU.mult), (over_heads(ln_b), ALU.add), (gates[buf][:, c], ALU.mult))):
                    if i > 0:
                        e.wait_ge(o_gated, 3 * n + i)
                        stand(e, pr.waits_passed)
                    e.tensor_tensor(on[:, :, :], on[:, :, :], b, op).then_inc(o_gated, 1)

            def a_round(r, buf, last=False):
                for c in range(TPB):
                    e.wait_ge(L_done, r * TPB + c + 1)
                    stand(e, pr.waits_passed)
                    e.tensor_tensor(R[:, c], negL[:, c], over_heads(pair), ALU.mult).then_inc(R_step, 1)
                    e.wait_ge(R_step, 2 * (r * TPB + c) + 1)
                    stand(e, pr.waits_passed)
                    e.tensor_tensor(R[:, c], R[:, c], over_heads(con["ident"]), ALU.add).then_inc(R_step, 1)
                    if c + 2 < TPB:
                        mask_gates(r, c + 2)
                if not last:
                    finish_projections(r + 1, 1 - buf)
                for c in range(TPB - 1):
                    gate_out(r, buf, c)
                if not last:
                    e.wait_ge(qS_done, (r + 1) * (TPB - 1))
                    stand(e, pr.waits_passed)
                    copy_tables(r + 1)
                    for c in range(2):
                        mask_gates(r + 1, c)
                gate_out(r, buf, TPB - 1)

            def first():
                copy_tables(0)
                for c in range(2):
                    mask_gates(0, c)
                finish_projections(0, 0)

            rounds(e, first, a_round, lambda r, buf: a_round(r, buf, last=True))

        @block.tensor
        def _(e):
            def piece(q, i, halves_=(0, 1)):
                for half in halves_:
                    if half == 0:
                        if i == 0:
                            e.wait_ge(xs_loaded, 16 * q + 16)
                        if i < 2:
                            e.wait_ge(conv_step, TAP_STEPS * (CONVS * q + i + 1))
                        elif i < TPB + 2:
                            e.wait_ge(g_copied, TPB * q + i - 1)
                        else:
                            e.wait_ge(conv_step, TAP_STEPS * (CONVS * q + i - TPB + 1))
                    for k in range(half * KD // 2, (half + 1) * KD // 2):
                        if i < TPB:
                            lhsT, rhs = xs[:, k, i * P:(i + 1) * P], w["g"][:, k, :]
                        else:
                            u = i - TPB
                            lhsT, rhs = w["kqv"[u // HG]][:, k, (u % HG) * DH:(u % HG + 1) * DH], xs[:, k, :]
                        mm = e.matmul(pj[i % 2][:, :], lhsT, rhs, start=(k == 0), stop=(k == KD - 1))
                mm.then_inc(pj_ready, 1) if halves_[-1] == 1 else None

            def turn_out(n, c):
                e.wait_ge(o_gated, 3 * n + 3)
                if c < TPB - 1:
                    e.wait_ge(ot_done, n + 2)
                for h in range(HG):
                    mm = e.transpose(d4[:, h, :], on[:, h, :], con["ident"][:, :])
                mm.then_inc(ot_ready, 1)

            def a_round(r, buf, last=False):
                qT, kT, vT = (heads[buf][m] for m in "qkv")
                chunk = lambda a, h, c: a[:, h, c * P:(c + 1) * P]
                after_first = not (isinstance(r, int) and r == 0)

                def next_piece(i, halves_=(0, 1)):
                    if not last:
                        piece(r + 1, i, halves_)

                e.wait_ge(silu_done, CONVS * r + CONVS + 2)
                e.wait_ge(k_scaled, HG * r + HG)
                for c in range(TPB):
                    n = r * TPB + c
                    if c > 0:
                        e.wait_ge(A_done, n)
                    elif after_first:
                        e.wait_ge(o_done, n)
                    for h in range(HG):
                        e.matmul(kk[:, h, :], chunk(kT, h, c), chunk(kT, h, c), start=True, stop=True)
                        mm = e.matmul(kq[:, h, :], chunk(kT, h, c), chunk(qT, h, c), start=True, stop=True)
                    mm.then_inc(kk_ready, 1)
                    e.wait_ge(la_masked, n + 1)
                    if c > 0:
                        e.wait_ge(decay_done, n)
                    elif after_first:
                        e.wait_ge(ot_done, n + 1)
                    e.matmul(d4, con["after"][:, :], masked_la[:, c % 2], start=True, stop=True).then_inc(d_ready, 1)
                    if c > 0:
                        e.wait_ge(kd_done, n)
                    for h in range(HG):
                        mm = e.transpose(r4[:, h, :], chunk(kT, h, c), con["ident"][:, :])
                    mm.then_inc(kt_ready, 1)
                    if c > 0:
                        e.wait_ge(v_done, n)
                    for h in range(HG):
                        mm = e.transpose(t4[:, h, :], chunk(vT, h, c), con["ident"][:, :])
                    mm.then_inc(vt_ready, 1)
                    next_piece(c)
                if after_first:
                    e.wait_ge(decay_done, r * TPB + TPB)
                    turn_out(r * TPB - 1, TPB - 1)
                for c in range(TPB):
                    n = r * TPB + c
                    e.wait_ge(R_step, 2 * n + 2)
                    if c > 0:
                        e.wait_ge(T_done, n)
                    for h in range(HG):
                        mm = e.transpose(z4[:, h, :], R[:, c, h, :], con["ident"][:, :])
                    mm.then_inc(rt_ready, 1)
                    if c < 2:
                        next_piece(TPB, (c,))

                for l, m in enumerate(LEVELS):
                    for c in range(TPB):
                        i = (r * NL + l) * TPB + c
                        if l == 0:
                            e.wait_ge(T_done, r * TPB + c + 1 if c >= 2 else r * TPB + TPB)
                        else:
                            e.wait_ge(tl_done, (r * (NL - 1) + l - 1) * TPB + c + 1)
                        if c >= 2 or l > 0:
                            e.wait_ge(zl_done, i - 1)
                        even, _odd = halves(T[:, c], m)
                        for h in range(HG):
                            mm = e.matmul(z_half[c % 2][:, h, :], negL[:, c, h, :], even[:, h], start=True, stop=True)
                        mm.then_inc(zl_ready, 1)
                        if c % 2 == 1:
                            next_piece(TPB + 1 + l, (c // 2,))
                    for c in range(TPB):
                        i = (r * NL + l) * TPB + c
                        e.wait_ge(zl_done, i + 1)
                        if l == 0 and c < 2:
                            e.wait_ge(kd_done, r * TPB + TPB)
                            e.wait_ge(v_done, r * TPB + TPB)
                        else:
                            e.wait_ge(rl_done, i - 1)
                        even, _odd = halves(Z[:, c], m)
                        _even, odd = halves(R[:, c], m)
                        for h in range(HG):
                            mm = e.matmul(r_half[c % 2][:, h, :], Z[:, c, h, :], odd[:, h], start=True, stop=True)
                        mm.then_inc(rl_ready, 1)
                        if m < P // 2:
                            j = (r * (NL - 1) + l) * TPB + c
                            if not (l == 0 and c < 2):
                                e.wait_ge(tl_done, j - 1)
                            for h in range(HG):
                                mm = e.matmul(t_half[c % 2][:, h, :], R[:, c, h, :], even[:, h], start=True, stop=True)
                            mm.then_inc(tl_ready, 1)

                for c in range(TPB):
                    n, m = r * TPB + c, r * (TPB - 1) + c
                    if c > 0:
                        e.wait_ge(S_done, HG * m)
                        if c == 1:
                            e.wait_ge(rl_done, (r + 1) * NL * TPB)
                        for h in range(HG):
                            mm = e.matmul(r4[:, h, :], chunk(kT, h, c), S[:, h, :], start=True, stop=True)
                        mm.then_inc(kS_ready, 1)
                        for h in range(HG):
                            mm = e.matmul(t4[:, h, :], chunk(qT, h, c), S[:, h, :], start=True, stop=True)
                        mm.then_inc(qS_ready, 1)
                    for i, half in (((11, 0),), ((12, 0), (12, 1)), ((13, 1),), ((15, 0),))[c]:
                        next_piece(i, (half,))
                    if c > 0:
                        e.wait_ge(v_less, HG * m)
                        e.wait_ge(err_done, n)
                    e.wait_ge(rl_done, (r * NL + NL - 1) * TPB + c + 1)
                    for h in range(HG):
                        mm = e.matmul(z4[:, h, :], R[:, c, h, :], negv[:, c, h, :], start=True, stop=True)
                    mm.then_inc(err_ready, 1)
                    for i, half in (((11, 1),), (), ((14, 0),), ((15, 1),))[c]:
                        next_piece(i, (half,))
                    e.wait_ge(err_done, n + 1)
                    if c < TPB - 1:
                        for h in range(HG):
                            mm = e.matmul(kq[:, h, :], kd[:, c, h, :], err[:, h, :], start=True, stop=True)
                        mm.then_inc(dS_ready, 1)
                    if c > 0:
                        e.wait_ge(o_done, n)
                    else:
                        e.wait_ge(rl_done, (r + 1) * NL * TPB)
                    for h in range(HG):
                        mm = e.matmul(kk[:, h, :], A[:, c, h, :], err[:, h, :], start=True, stop=True)
                    mm.then_inc(Ae_ready, 1)
                    for i, half in ((), ((13, 0),), ((14, 1),), ())[c]:
                        next_piece(i, (half,))
                    if c > 0:
                        turn_out(n - 1, c - 1)

            def first():
                for i in range(NP):
                    piece(0, i)

            def tail(r, buf):
                a_round(r, buf, last=True)
                e.wait_ge(ot_done, r * TPB + TPB + 1)
                turn_out(r * TPB + TPB - 1, TPB - 1)

            rounds(e, first, a_round, tail)

        @block.scalar
        def _(e):
            def gate(q, buf, c):
                e.wait_ge(pj_ready, NP * q + c + 1)
                e.activation(gates[buf][:, c], p4[c % 2], ACT.Tanh, scale=0.5).then_inc(g_copied, 1)

            def tap(q, u):
                m, h = "kqv"[u // HG], u % HG
                e.wait_ge(pj_ready, NP * q + TPB + u + 1)
                e.wait_ge(silu_done, CONVS * q + u + 1)
                e.activation(conv[:, u % 2, :], pj[u % 2][:, :], ACT.Identity, bias=conv_b[m][:, h:h + 1],
                             scale=conv_w[m][:, h, TAPS - 1:TAPS]).then_inc(tap_done, 1)

            def silu(q, buf, u):
                e.wait_ge(conv_step, TAP_STEPS * (CONVS * q + u + 3))
                e.activation(heads[buf]["kqv"[u // HG]][:, u % HG, :], conv[:, u % 2, :], ACT.Silu).then_inc(silu_done, 1)

            def store(n, dst):
                e.wait_ge(ot_ready, n + 1)
                e.wait_ge(ot_stored, 16 * n + 16)
                e.activation(oT[:, :, :], d4, ACT.Copy).then_inc(ot_done, 1)
                e.wait_ge(ot_done, n + 3)
                stand(e, pr.waits_passed)
                e.dma_start(dst, oT[:, :, :]).then_inc(ot_stored, 16)

            ot_round = io["ot_d"].rearrange("g b c p h m -> (g b) c p h m")

            def a_round(r, buf, last=False):
                after_first = not (isinstance(r, int) and r == 0)
                next_tap = lambda u: None if last else tap(r + 1, u)
                next_silu = lambda u: None if last else silu(r + 1, 1 - buf, u)
                e.preload_act_table_set("exp_and_others")
                for c in range(TPB):
                    n = r * TPB + c
                    e.wait_ge(d_ready, n + 1)
                    if c > 0:
                        e.wait_ge(G_done, n)
                    e.activation(decay[:, :, :], d4, ACT.Exp).then_inc(decay_done, 1)
                    e.wait_ge(vt_ready, n + 1)
                    e.activation(negv[:, c], t4, ACT.Copy, scale=-1.0).then_inc(v_done, 1)
                    if not last:
                        gate(r + 1, 1 - buf, c)
                if after_first:
                    store(r * TPB - 1, ot_round[r - 1, TPB - 1])
                e.preload_act_table_set("silu_and_others")
                for c in range(TPB):
                    e.wait_ge(rt_ready, r * TPB + c + 1)
                    e.activation(T[:, c], z4, ACT.Copy).then_inc(T_done, 1)
                next_tap(0)
                for l, m in enumerate(LEVELS):
                    for c in range(TPB):
                        i = (r * NL + l) * TPB + c
                        e.wait_ge(zl_ready, i + 1)
                        even, _odd = halves(Z[:, c], m)
                        e.activation(even, z_half[c % 2].rearrange("p h (n m) -> p h n m", m=m), ACT.Copy).then_inc(zl_done, 1)
                    next_tap(l + 1)
                    next_silu(l)
                for c in range(TPB):
                    n = r * TPB + c
                    if c == 2:
                        next_tap(9)
                    e.wait_ge(err_ready, n + 1)
                    e.activation(err[:, :, :], z4, ACT.Copy, scale=-1.0).then_inc(err_done, 1)
                    if c != 2:
                        next_tap((7, 8, None, 11)[c])
                    next_silu((6, 7, 8, 10)[c])
                    if c > 0:
                        store(n - 1, ot_round[r, c - 1])
                    if c == 2:
                        next_tap(10)
                        next_silu(9)
                next_silu(11)

            def first():
                e.preload_act_table_set("silu_and_others")
                for c in range(TPB):
                    gate(0, 0, c)
                for u in range(CONVS):
                    tap(0, u)
                    if u > 0:
                        silu(0, 0, u - 1)
                silu(0, 0, CONVS - 1)

            def tail(r, buf):
                a_round(r, buf, last=True)
                store(r * TPB + TPB - 1, ot_round[r, TPB - 1])

            rounds(e, first, a_round, tail)
            e.wait_ge(ot_stored, 16 * NR * TPB + 16)

        @block.vector
        def _(e):
            e.wait_ge(cleared, 2)

            def taps(q, u):
                m, h = "kqv"[u // HG], u % HG
                e.wait_ge(tap_done, CONVS * q + u + 1)
                for s in range(1, TAPS):
                    if s > 1:
                        e.wait_ge(conv_step, (CONVS * q + u + 2) * TAP_STEPS + s - 1)
                    oc = conv[:, u % 2, s:SEQ]
                    e.scalar_tensor_tensor(oc, pj[u % 2][:, 0:SEQ - s], conv_w[m][:, h, TAPS - 1 - s:TAPS - s], oc,
                                           ALU.mult, ALU.add).then_inc(conv_step, 1)

            def norm_out(n, c):
                e.wait_ge(o_done, n + 1)
                for h in range(HG):
                    e.bn_stats(o_st[:, h, :], o[:, c % 2, h, :]).then_inc(o_stats, 1)
                e.wait_ge(o_stats, HG * n + HG)
                stand(e, pr.waits_passed)
                for h in range(HG):
                    e.bn_aggr(o_mv[:, h, :], o_st[:, h, :]).then_inc(o_mean, 1)
                e.wait_ge(o_mean, HG * n + HG)
                ve, t, g = o_ve[:, :], o_t[:, :], o_rs[:, :]
                step = n * RSTD_STEPS
                e.tensor_scalar(ve, o_mv[:, :, 1], EPS, None, ALU.add).then_inc(o_rstd, 1)
                e.wait_ge(o_rstd, step + 1)
                e.tensor_scalar(t.bitcast(I32), ve.bitcast(I32), 1, None, ALU.arith_shift_right).then_inc(o_rstd, 1)
                e.wait_ge(o_rstd, step + 2)
                e.tensor_scalar(g.bitcast(I32), t.bitcast(I32), -1.0, float(0x5f3759df), ALU.mult, ALU.add).then_inc(o_rstd, 1)
                for i in range(3):
                    e.wait_ge(o_rstd, step + 4 * i + 3)
                    e.tensor_tensor(t, g, g, ALU.mult).then_inc(o_rstd, 1)
                    e.wait_ge(o_rstd, step + 4 * i + 4)
                    e.tensor_tensor(t, t, ve, ALU.mult).then_inc(o_rstd, 1)
                    e.wait_ge(o_rstd, step + 4 * i + 5)
                    e.tensor_scalar(t, t, -0.5, 1.5, ALU.mult, ALU.add).then_inc(o_rstd, 1)
                    e.wait_ge(o_rstd, step + 4 * i + 6)
                    e.tensor_tensor(g, g, t, ALU.mult).then_inc(o_rstd, 1)
                e.wait_ge(o_rstd, step + RSTD_STEPS)
                if not (isinstance(n, int) and n == 0):
                    e.wait_ge(ot_ready, n)
                for h in range(HG):
                    e.tensor_scalar(on[:, h, :], o[:, c % 2, h, :], o_mv[:, h, 0:1], o_rs[:, h:h + 1],
                                    ALU.subtract, ALU.mult).then_inc(o_normed, 1)

            def a_round(r, buf, last=False):
                next_taps = lambda u: None if last else taps(r + 1, u)
                for c in range(TPB):
                    n = r * TPB + c
                    e.wait_ge(decay_done, n + 1)
                    e.wait_ge(b_masked, n + 1)
                    e.tensor_tensor(G[:, c % 2], decay[:, :, :], masked_b[:, c % 2], ALU.mult).then_inc(G_done, 1)
                    e.wait_ge(G_done, n + 1)
                    e.wait_ge(kk_ready, n + 1)
                    e.scalar_tensor_tensor(negL[:, c, :, 1:P], kk[:, :, 1:P], -1.0, G[:, c % 2, :, 0:P - 1],
                                           ALU.mult, ALU.mult).then_inc(L_done, 1)
                    e.tensor_tensor(A[:, c], kq, G[:, c % 2], ALU.mult).then_inc(A_done, 1)
                    e.wait_ge(kt_ready, n + 1)
                    e.tensor_tensor(kd[:, c], r4, G[:, c % 2, :, P - 1:P].to_broadcast(H4), ALU.mult).then_inc(kd_done, 1)
                next_taps(0)
                for l, m in enumerate(LEVELS):
                    for c in range(TPB):
                        i = (r * NL + l) * TPB + c
                        j = (r * (NL - 1) + l) * TPB + c
                        as_blocks = lambda a: a.rearrange("p h (n m) -> p h n m", m=m)
                        wide = lambda a: a[:, :].bitcast(U32).rearrange("p (n m) -> p n m", m=m).unsqueeze(1).to_broadcast([P, HG, P // 2 // m, m])
                        e.wait_ge(rl_ready, i + 1)
                        if m < P // 2:
                            e.wait_ge(tl_ready, j + 1)
                        stand(e, pr.waits_passed)
                        _even, odd = halves(R[:, c], m)
                        e.copy_predicated(odd, wide(mask_R[l]), as_blocks(r_half[c % 2])).then_inc(rl_done, 1)
                        if m < P // 2:
                            even, _odd = halves(T[:, c], m)
                            e.copy_predicated(even, wide(mask_T[l]), as_blocks(t_half[c % 2])).then_inc(tl_done, 1)
                    next_taps(l + 1)
                for c in range(TPB):
                    n, m = r * TPB + c, r * (TPB - 1) + c
                    oc = o[:, c % 2]
                    if c > 0:
                        e.wait_ge(kS_ready, m)
                        e.wait_ge(v_done, n + 1)
                        for h in range(HG):
                            e.scalar_tensor_tensor(negv[:, c, h, :], r4[:, h, :], before[:, c, h:h + 1], negv[:, c, h, :],
                                                   ALU.mult, ALU.add).then_inc(v_less, 1)
                        e.wait_ge(qS_ready, m)
                        e.tensor_tensor(oc, t4, on_heads(upto, c), ALU.mult).then_inc(qS_done, 1)
                        norm_out(n - 1, c - 1)
                    if c < TPB - 1:
                        e.wait_ge(dS_ready, m + 1)
                        if c == 0:
                            e.tensor_copy(S[:, :, :], kq).then_inc(S_done, HG)
                        else:
                            for h in range(HG):
                                e.scalar_tensor_tensor(S[:, h, :], S[:, h, :], whole[:, c, h:h + 1], kq[:, h, :],
                                                       ALU.mult, ALU.add).then_inc(S_done, 1)
                    else:
                        next_taps(10)
                    e.wait_ge(Ae_ready, n + 1)
                    if c == 0:
                        e.tensor_copy(oc, kk).then_inc(o_done, 1)
                    else:
                        e.wait_ge(qS_done, m)
                        e.tensor_tensor(oc, oc, kk, ALU.add).then_inc(o_done, 1)
                    next_taps((7, 8, 9, 11)[c])
                norm_out(r * TPB + TPB - 1, TPB - 1)

            def first():
                for u in range(CONVS):
                    taps(0, u)

            rounds(e, first, a_round, lambda r, buf: a_round(r, buf, last=True))


def phase_delta_out(pr, con, XT, route_part):
    nc, io = pr.nc, pr.io
    with ExitStack() as st:
        sb = lambda n, s: pr.sb(st, "d_" + n, s)
        ps = lambda n, s: pr.ps(st, "d_ps_" + n, s)
        sem = lambda n: pr.sem("d_" + n)
        n = Norm(pr, st, "d")
        w_o = sb("w_o", [P, NH, DM])
        heads = sb("heads", [P, TPB, NH, P])
        switch = sb("switch", [P, NE, TPB * DM])
        products = sb("products", [P, TPB * DM])
        part = sb("part", [P, NE])
        y = sb("y", [P, TPB, DM])
        yo = [ps(f"yo{i}", [P, DM]) for i in range(2)]
        turned = ps("tp", [P, KD, P])
        wo_loaded, switch_loaded = sem("wo_loaded"), sem("switch_loaded")
        heads_loaded = [sem(f"heads_loaded{c}") for c in range(TPB)]
        yo_ready = sem("yo_ready")
        y_free = sem("y_free")
        switched = sem("switched")
        part_kept = sem("part_kept")
        block = st.enter_context(nc.Block())

        @block.sync
        def _(e):
            e.dma_start(w_o[:, :, :], io["w_o"]).then_inc(wo_loaded, 16)
            with e.Fori(0, NB) as b:
                for c in range(TPB):
                    e.wait_ge(yo_ready, b * TPB + c + 1)
                    stand(e, pr.waits_passed)
                    e.dma_start(heads[:, c, :, :].rearrange("p (g h) m -> p g h m", h=HG),
                                io["ot_d"].rearrange("g b c p h m -> b c p g h m")[b, c]).then_inc(heads_loaded[c], 16)
                norm_sync(e, n, b, rows(io["x2"], b), rows(io["x3"], b))
            e.wait_ge(n.x_stored, 16 * NB + 1)

        @block.gpsimd
        def _(e):
            norm_start(e, n)
            for s, k in ((yo_ready, TPB), (y_free, 2), (switched, 1), (part_kept, 1)):
                e.sem_inc(s, k)
            e.dma_start(switch[:, :, :], io["switch_w"]).then_inc(switch_loaded, 16)

        @block.tensor
        def _(e):
            e.wait_ge(wo_loaded, 16)
            with e.Fori(0, NB) as b:
                for c in range(TPB):
                    e.wait_ge(heads_loaded[c], 16 * b + 16)
                    e.wait_ge(y_free, b * TPB + c + 1)
                    for h in range(NH):
                        mm = e.matmul(yo[c % 2][:, :], heads[:, c, h, :], w_o[:, h, :], start=(h == 0), stop=(h == NH - 1))
                    mm.then_inc(yo_ready, 1)
                norm_x_tensor(e, n, b, turned, con["ident"][:, :])

        @block.scalar
        def _(e):
            with e.Fori(0, NB) as b:
                for c in range(TPB):
                    e.wait_ge(yo_ready, b * TPB + c + TPB + 1)
                    e.activation(y[:, c, :], yo[c % 2][:, :], ACT.Copy).then_inc(y_free, 1)
                norm_y_scalar(e, n, b, con["eps"][:, :])
                norm_x_scalar(e, n, b, con["eps"][:, :], turned, lambda c: XT[:, b, :, c * P:(c + 1) * P])

        @block.vector
        def _(e):
            with e.Fori(0, NB) as b:
                norm_y_vector(e, n, b, lambda c: y[:, c, :], lambda c: e.wait_ge(y_free, b * TPB + c + 3))
                norm_x_vector(e, n, b, lambda c: e.wait_ge(n.x_new, TPB * b + c + 1))
                e.wait_ge(switch_loaded, 16)
                e.wait_ge(n.x_normed, TPB * b + TPB + 1)
                e.wait_ge(part_kept, b + 1)
                for x in range(NE):
                    e.wait_ge(switched, NE * b + x + 1)
                    e.scalar_tensor_tensor(products[:, :], n.yn[:, :, :].rearrange("p c d -> p (c d)"), 1.0, switch[:, x, :],
                                           ALU.mult, ALU.mult, accum_out=part[:, x:x + 1]).then_inc(switched, 1)
                e.wait_ge(switched, NE * b + NE + 1)
                e.tensor_copy(route_part[:, b, :], part[:, :]).then_inc(part_kept, 1)


def phase_experts(pr, con, XT, route_part):
    nc, io = pr.nc, pr.io
    HB = P // FH
    with ExitStack() as st:
        sb = lambda n, s: pr.sb(st, "e_" + n, s)
        ps = lambda n, s: pr.ps(st, "e_ps_" + n, s)
        sem = lambda n: pr.sem("e_" + n)
        n = Norm(pr, st, "e")
        shape = [P, NB, NE]
        t = route_tiles(lambda k, s: sb("r_" + k, s), NB)
        switch_b = sb("switch_b", [P, NE])
        w1, w2 = sb("w1", [P, FH, NE]), sb("w2", [P, FH, NE])
        b1, b2 = sb("b1", [P, NE]), sb("b2", [P, NE])
        w3, b3 = sb("w3", [P, KD, DM]), sb("b3", [P, DM])
        chosen = [sb(f"chosen{i}", [P, FH, NE]) for i in range(2)]
        w1_sel, w2_sel = sb("w1_sel", [P, NB, 2, FH]), sb("w2_sel", [P, NB, 2, FH])
        b1_sel, b2_sel = sb("b1_sel", [P, NB, 2]), sb("b2_sel", [P, NB])
        same_head = sb("same_head", [P, P])
        w1_diag, w2_diag = sb("w1_diag", [P, 2, HB, FH]), sb("w2_diag", [P, 2, HB, FH])
        hidden = sb("hidden", [P, 2, 2, SEQ])
        mixed = sb("mixed", [P, KD, SEQ])
        y = sb("y", [P, TPB, DM])
        l_ps = ps("logits", [P, NB, NE])
        h_ps = [ps(f"h{i}", [P, SEQ]) for i in range(2)]
        o_ps = [ps(f"o{i}", [P, SEQ]) for i in range(2)]
        y_ps = [ps(f"y{i}", [P, DM]) for i in range(2)]
        loaded = sem("loaded")
        masks = sem("masks")
        route = sem("route")
        logits_ready = sem("logits_ready")
        diag_done = sem("diag_done")
        h_ready = sem("h_ready")
        gelu_done = sem("gelu_done")
        o_ready = sem("o_ready")
        mixed_done = sem("mixed_done")
        y_ready, y_done = sem("y_ready"), sem("y_done")
        block = st.enter_context(nc.Block())

        @block.sync
        def _(e):
            for dst, name in ((w1, "w1"), (w2, "w2"), (b1, "b1"), (b2, "b2"), (w3, "w3")):
                e.dma_start(dst[:], io[name]).then_inc(loaded, 16)
            e.dma_start(switch_b[:, :], io["switch_b"].partition_broadcast(P)).then_inc(loaded, 16)
            e.dma_start(b3[:, :], io["b3"].partition_broadcast(P)).then_inc(loaded, 16)
            with e.Fori(0, NB) as b:
                norm_sync(e, n, b, rows(io["x3"], b), rows(io["out"], b))
            e.wait_ge(n.x_stored, 16 * NB + 1)

        @block.gpsimd
        def _(e):
            norm_start(e, n)
            e.sem_inc(n.x_normed, NB * TPB)
            e.sem_inc(n.turned, NB * TPB)
            for s, k in ((route, 1), (gelu_done, 2), (mixed_done, 2), (y_done, 2)):
                e.sem_inc(s, k)
            for x in range(NE):
                e.memset(t["prefer"][:, x:x + 1], float(NE - x)).then_inc(masks, 1)
            e.memset(same_head[:, :], 0.0).then_inc(masks, 1)
            e.wait_ge(masks, NE + 1)
            for j in range(HB):
                e.memset(same_head[j * FH:(j + 1) * FH, j * FH:(j + 1) * FH], 1.0).then_inc(masks, 1)

        @block.tensor
        def _(e):
            e.matmul(l_ps[:, :, :], con["ones"][:, :], route_part[:, :, :], start=True, stop=True).then_inc(logits_ready, 1)
            e.wait_ge(loaded, 16 * 7)
            with e.Fori(0, NB) as b:
                def hidden_layer(dc):
                    for k in range(2):
                        e.wait_ge(gelu_done, 8 * b + 2 * dc + k + 1)
                        e.matmul(h_ps[k][:, :], w1_diag[:, k].rearrange("p j f -> p (j f)"), XT[:, b, dc, :],
                                 start=True, stop=True).then_inc(h_ready, 1)

                def output_layer(dc):
                    e.wait_ge(mixed_done, KD * b + dc + 1)
                    for k in range(2):
                        e.wait_ge(gelu_done, 8 * b + 2 * dc + k + 3)
                        mm = e.matmul(o_ps[dc % 2][:, :], w2_diag[:, k].rearrange("p j f -> p (j f)"), hidden[:, dc % 2, k, :],
                                      start=(k == 0), stop=(k == 1))
                    mm.then_inc(o_ready, 1)

                e.wait_ge(diag_done, 4 * b + 4)
                hidden_layer(0)
                for dc in range(1, KD):
                    hidden_layer(dc)
                    output_layer(dc - 1)
                output_layer(KD - 1)
                e.wait_ge(mixed_done, KD * b + KD + 2)
                for c in range(TPB):
                    e.wait_ge(y_done, TPB * b + c + 1)
                    for k in range(KD):
                        mm = e.matmul(y_ps[c % 2][:, :], mixed[:, k, c * P:(c + 1) * P], w3[:, k, :],
                                      start=(k == 0), stop=(k == KD - 1))
                    mm.then_inc(y_ready, 1)

        @block.scalar
        def _(e):
            e.wait_ge(route, 4)
            e.activation(t["score"][:, :, :], t["score"][:, :, :], ACT.Exp).then_inc(route, 1)
            with e.Fori(0, NB) as b:
                for dc in range(KD):
                    for k in range(2):
                        e.wait_ge(h_ready, 8 * b + 2 * dc + k + 1)
                        stand(e, pr.waits_passed)
                        e.activation(hidden[:, dc % 2, k, :], h_ps[k][:, :], ACT.Gelu,
                                     bias=b1_sel[:, :, :].unsqueeze(3)[:, b, k, :]).then_inc(gelu_done, 1)
                norm_y_scalar(e, n, b, con["eps"][:, :])

        @block.vector
        def _(e):
            e.wait_ge(loaded, 16 * 7)
            e.wait_ge(masks, NE + 1 + HB)
            e.wait_ge(logits_ready, 1)
            e.tensor_tensor(t["rest"][:, :, :], l_ps[:, :, :], switch_b[:, :].unsqueeze(1).to_broadcast(shape), ALU.add).then_inc(route, 1)
            m = softmax_front(e, t["rest"][:, :, :], t, shape, route, 2)
            m = softmax_back(e, t, shape, route, m + 1)
            m = top2(e, t["score"][:, :, :], shape, t, route, m)
            e.wait_ge(route, m)
            for one, gated in (("one1", "key"), ("one2", "rest")):
                e.tensor_tensor(t[gated][:, :, :], t[one][:, :, :], t["score"][:, :, :], ALU.mult).then_inc(route, 1)
            m += 2
            e.wait_ge(route, m)

            def choose(dst, table, row, step):
                i = step % 2
                e.wait_ge(route, step)
                e.tensor_tensor(chosen[i][:, :, :], table[:, :, :], row.unsqueeze(1).to_broadcast([P, FH, NE]), ALU.mult).then_inc(route, 1)
                e.wait_ge(route, step + 1)
                e.tensor_reduce(dst, chosen[i][:, :, :], AX.X, ALU.add).then_inc(route, 1)
                return step + 2

            def choose_bias(dst, table, row, step):
                e.wait_ge(route, step)
                e.tensor_tensor(chosen[0][:, 0, :], table[:, :], row, ALU.mult).then_inc(route, 1)
                e.wait_ge(route, step + 1)
                e.tensor_reduce(dst, chosen[0][:, 0, :], AX.X, ALU.add).then_inc(route, 1)
                return step + 2

            for b in range(NB):
                for k, (one, gated) in enumerate((("one1", "key"), ("one2", "rest"))):
                    m = choose(w1_sel[:, b, k, :], w1, t[one][:, b, :], m)
                    m = choose(w2_sel[:, b, k, :], w2, t[gated][:, b, :], m)
                    m = choose_bias(b1_sel[:, b, k:k + 1], b1, t[one][:, b, :], m)
                e.wait_ge(route, m)
                e.tensor_tensor(t["score"][:, b, :], t["key"][:, b, :], t["rest"][:, b, :], ALU.add).then_inc(route, 1)
                m = choose_bias(b2_sel[:, b:b + 1], b2, t["score"][:, b, :], m + 1)
            e.wait_ge(route, m)
            heads4 = same_head[:, :].rearrange("p (j f) -> p j f", j=HB)
            with e.Fori(0, NB) as b:
                for sel, diag in ((w1_sel, w1_diag), (w2_sel, w2_diag)):
                    for k in range(2):
                        e.tensor_tensor(diag[:, k], heads4, sel[:, b, k, :].unsqueeze(1).to_broadcast([P, HB, FH]), ALU.mult).then_inc(diag_done, 1)
                for dc in range(KD):
                    e.wait_ge(o_ready, KD * b + dc + 1)
                    e.scalar_tensor_tensor(mixed[:, dc, :], o_ps[dc % 2][:, :], b2_sel[:, :].unsqueeze(2)[:, b, :], XT[:, b, dc, :],
                                           ALU.add, ALU.add).then_inc(mixed_done, 1)
                for c in range(TPB):
                    e.wait_ge(y_ready, TPB * b + c + 1)
                    e.tensor_tensor(y[:, c, :], y_ps[c % 2][:, :], b3[:, :], ALU.add).then_inc(y_done, 1)
                norm_y_vector(e, n, b, lambda c: y[:, c, :], lambda c: e.wait_ge(y_done, TPB * b + c + 3))


def program(nc, io):
    for name in ("x1", "x2", "x3"):
        io[name] = nc.dram_tensor(name, [NB, SEQ, DM], F32).ap()
    io["xt_d"] = nc.dram_tensor("xt_d", [NB, P, KD, SEQ], F32).ap()
    io["ot_d"] = nc.dram_tensor("ot_d", [NG, NB, TPB, P, HG, P], F32).ap()
    pr = Program(nc, io)
    with pr.lasting as lasting:
        con = constants(pr, lasting)
        with ExitStack() as first:
            tab = gate_tables(pr, first)
            with ExitStack() as st:
                XT = pr.sb(st, "XT", [P, NB, KD, SEQ])
                phase_first_norm(pr, con, XT)
                phase_ssm(pr, con, XT)
                pr.retire_sems()
                phase_moe(pr, con, XT)
                phase_gates(pr, con, XT, tab)
            phase_delta(pr, con, tab)
        pr.retire_sems()
        XT = pr.sb(lasting, "XT2", [P, NB, KD, SEQ])
        route_part = pr.sb(lasting, "route_part", [P, NB, NE])
        phase_delta_out(pr, con, XT, route_part)
        phase_experts(pr, con, XT, route_part)


def host_layout(d):
    import numpy as np
    col = lambda a: np.ascontiguousarray(np.asarray(a).reshape(CT, P).T)
    chunks = lambda a: np.ascontiguousarray(np.asarray(a).reshape(-1, P, np.shape(a)[-1]).transpose(1, 0, 2))
    g = {k: np.asarray(v) for k, v in d.items()}
    o = {}
    o["x"] = g["L0_attn_hidden_states"]
    o["w_in"] = chunks(g["L0_attn_in_proj_w"].T)
    o["w_gate"] = chunks(g["L0_attn_gate_proj_w"].T)
    o["w_out"] = chunks(g["L0_attn_out_proj_w"].T)
    o["conv_w"] = np.ascontiguousarray(g["L0_attn_conv_weight"].reshape(CT, P, TAPS).transpose(1, 0, 2))
    o["conv_b"] = col(g["L0_attn_conv_bias"])
    o["dt_w"] = col(g["L0_attn_dt_w"])
    o["dt_b"] = col(np.repeat(g["L0_attn_dt_b"], 64))
    o["a_log"] = col(g["L0_attn_A_log"])
    o["col_b"], o["col_c"], o["col_d"] = col(g["L0_attn_B"]), col(g["L0_attn_C"]), col(g["L0_attn_D"])
    sgu, sdn = g["L0_ffn_shared_gate_up"], g["L0_ffn_shared_down"]
    fs = NSH * FE
    gu = np.concatenate([g["L0_ffn_gate_up_weights"]] + [
        np.concatenate([sgu[i * FE:(i + 1) * FE], sgu[fs + i * FE:fs + (i + 1) * FE]])[None] for i in range(NSH)])
    o["w_gu"] = np.ascontiguousarray(gu.transpose(0, 2, 1).reshape(NX, KD, P, 2 * FE).transpose(0, 2, 1, 3))
    dn = np.concatenate([g["L0_ffn_down_weights"]] + [sdn[None, :, i * FE:(i + 1) * FE] for i in range(NSH)])
    rows_in = np.zeros((NX, len(FT) * P, DM), dn.dtype)
    rows_in[:, :FE] = dn.transpose(0, 2, 1)
    o["w_dn"] = np.ascontiguousarray(rows_in.reshape(NX, len(FT), P, DM).transpose(0, 2, 1, 3))
    o["gate_w"] = chunks(g["L0_ffn_gate_weight"].T)
    for m in "qkvg":
        wm = g["L1_attn_W" + m].reshape(KD, P, NG, HG * DH)
        o["w_" + m] = np.ascontiguousarray(wm.transpose(2, 1, 0, 3))
    for m in "qkv":
        o["conv_w" + m] = np.ascontiguousarray(g[f"L1_attn_{m}cw"].reshape(NG, HG, DH, TAPS).transpose(0, 2, 1, 3))
        o["conv_b" + m] = np.ascontiguousarray(g[f"L1_attn_{m}cb"].reshape(NG, HG, DH).transpose(0, 2, 1))
    o["w_ab"] = chunks(np.concatenate([g["L1_attn_Wa"], g["L1_attn_Wb"]], 1))
    o["b_ab"] = np.concatenate([g["L1_attn_ba"], g["L1_attn_bb"]])
    o["ln_w"], o["ln_b"] = g["L1_attn_ln_w"], g["L1_attn_ln_b"]
    o["w_o"] = chunks(g["L1_attn_Wo"])
    o["switch_w"] = np.ascontiguousarray(g["L1_ffn_switch_w"].reshape(NE, TPB, P, DM).transpose(2, 0, 1, 3).reshape(P, NE, TPB * DM))
    o["switch_b"], o["b3"] = g["L1_ffn_switch_b"], g["L1_ffn_b3"]
    per_head = lambda a: np.ascontiguousarray(np.tile(a, (P // FH,) + (1,) * (a.ndim - 1)))
    o["w1"], o["w2"] = per_head(g["L1_ffn_w1"].transpose(2, 1, 0)), per_head(g["L1_ffn_w2"].transpose(2, 1, 0))
    o["b1"], o["b2"] = per_head(g["L1_ffn_b1"].T), per_head(g["L1_ffn_b2"].T)
    o["w3"] = chunks(g["L1_ffn_w3"].T)
    return o


def kernel(**inputs):
    import numpy as np
    import concourse.bacc as bacc
    from concourse.bass_utils import run_bass_kernel_spmd

    nc = bacc.Bacc("TRN2", target_bir_lowering=False, num_devices=1)
    arrays, io = {}, {}
    for name, a in host_layout(inputs).items():
        a = np.ascontiguousarray(a)
        arrays[f"in_{name}"] = a
        io[name] = nc.dram_tensor(f"in_{name}", a.shape, mybir.dt.from_np(a.dtype), kind="ExternalInput").ap()
    io["out"] = nc.dram_tensor("out", [NB, SEQ, DM], F32, kind="ExternalOutput").ap()
    program(nc, io)
    r = run_bass_kernel_spmd(nc, [arrays], core_ids=[0])
    return r.results[0]["out"]
```
